# Optimizing a Trainium2 kernel written in Bass

```python
import numpy as np
import jax
import jax.numpy as jnp

def _softmax(x, axis=-1):
    return jax.nn.softmax(x, axis=axis)

def _gelu(x):
    return jax.nn.gelu(x, approximate=True)

def _silu(x):
    return jax.nn.silu(x)

def _sigmoid(x):
    return jax.nn.sigmoid(x)

def _layernorm(x, axis=-1, eps=1e-05):
    m = jnp.mean(x, axis=axis, keepdims=True)
    v = jnp.var(x, axis=axis, keepdims=True)
    return (x - m) / jnp.sqrt(v + eps)

def _scatter_add(tgt, idx, src, axis=0):
    return tgt.at[idx].add(src)

def _segment_sum(src, seg, n):
    return jax.ops.segment_sum(src, seg, n)
kernel_name = 'mk_adj_ffn_d2_adj_r2_109749'

def setup_inputs(seed: int=0):
    np.random.seed(seed)
    _w = jnp.asarray

    def _rec_inputs():
        import jax
        import jax.numpy as jnp
        _gk = jax.random.key(seed)
        x = 7.22e-05 + 1 * jax.random.normal(jax.random.fold_in(_gk, 1), (16, 512, 128), jnp.float32)
        _w = (1.0 + jnp.arange(512, dtype=jnp.float32)) ** (-0.5)
        _w = _w / _w.mean()
        _pij = jnp.clip(0.015625 * _w[:, None] * _w[None, :], 0.0, 1.0)
        _a = jax.random.uniform(jax.random.fold_in(_gk, 2), (16, 512, 512)) < _pij
        _a = jnp.logical_or(_a, jnp.swapaxes(_a, -1, -2))
        _a = jnp.logical_or(_a, jnp.eye(512, dtype=bool))
        _af = _a.astype(jnp.float32)
        _af = _af * jax.random.uniform(jax.random.fold_in(_gk, 3), (16, 512, 512), jnp.float32, 0.05, 1)
        adj = _af
        _nm = jnp.ones((16, 512), dtype=bool)
        nodemask = jnp.where(_nm, 1.0, 0.0).astype(jnp.float32)
        return (x, adj, nodemask)
    x, adj, nodemask = _rec_inputs()

    def _L0_gnn_setup():
        import jax, jax.numpy as jnp
        import numpy as np
        B, N, F_IN, F_OUT = (32, 512, 128, 128)
        EPS = 1e-08
        key = jax.random.key(seed)
        k1, k2, k3 = jax.random.split(key, 3)
        x = jax.random.normal(k1, (B, N, F_IN), dtype=jnp.float32)
        adj = jax.random.uniform(k2, (B, N, N), dtype=jnp.float32)
        fan_in, fan_out = (2 * F_IN, F_OUT)
        limit = float(np.sqrt(6.0 / (fan_in + fan_out)))
        weight = jax.random.uniform(k3, (2 * F_IN, F_OUT), minval=-limit, maxval=limit, dtype=jnp.float32)
        bias = jnp.zeros((F_OUT,), dtype=jnp.float32)
        return {'x': x, 'adj': adj, 'weight': weight, 'bias': bias}
    _L0_gnn_all = _L0_gnn_setup()
    _L0_gnn_in = {k: v for k, v in _L0_gnn_all.items() if k in ('weight', 'bias')}
    del _L0_gnn_all

    def _L0_ffn_setup():
        import jax, jax.numpy as jnp
        import numpy as np
        B, K, D = (256, 16, 128)
        E = 32
        H = int(D * 0.25)
        key = jax.random.key(seed)
        ks = jax.random.split(key, 7)
        d_rs = D ** (-0.5)
        h_rs = H ** (-0.5)
        x = jax.random.normal(ks[0], (B, K, D), dtype=jnp.float32)
        router_w = jax.random.uniform(ks[1], (E, D), jnp.float32, -d_rs, d_rs)
        router_b = jax.random.uniform(ks[2], (E,), jnp.float32, -d_rs, d_rs)
        W1 = jax.random.uniform(ks[3], (E, D, H), jnp.float32, -h_rs, h_rs)
        b1 = jax.random.uniform(ks[4], (E, H), jnp.float32, -h_rs, h_rs)
        W2 = jax.random.uniform(ks[5], (E, H, D), jnp.float32, -d_rs, d_rs)
        b2 = jax.random.uniform(ks[6], (E, D), jnp.float32, -d_rs, d_rs)
        return {'x': x, 'router_w': router_w, 'router_b': router_b, 'W1': W1, 'b1': b1, 'W2': W2, 'b2': b2}
    _L0_ffn_all = _L0_ffn_setup()
    _L0_ffn_in = {k: v for k, v in _L0_ffn_all.items() if k in ('router_w', 'router_b', 'W1', 'b1', 'W2', 'b2')}
    del _L0_ffn_all

    def _L1_gnn_setup():
        import jax, jax.numpy as jnp
        import numpy as np
        B, N, IN_DIM, OUT_DIM = (8, 1024, 128, 128)
        EDGE_P = 0.02
        MASK_P = 0.9
        key = jax.random.key(seed)
        ks = jax.random.split(key, 8)
        x = jax.random.normal(ks[0], (B, N, IN_DIM), dtype=jnp.float32)
        adj = (jax.random.uniform(ks[1], (B, N, N)) < EDGE_P).astype(jnp.float32)
        mask = (jax.random.uniform(ks[2], (B, N)) < MASK_P).astype(jnp.float32)
        lim1 = 1.0 / np.sqrt(IN_DIM)
        W = jax.random.uniform(ks[3], (OUT_DIM, IN_DIM), minval=-lim1, maxval=lim1, dtype=jnp.float32)
        b = jax.random.uniform(ks[4], (OUT_DIM,), minval=-lim1, maxval=lim1, dtype=jnp.float32)
        lim2 = 1.0 / np.sqrt(2 * OUT_DIM)
        a1 = jax.random.uniform(ks[5], (OUT_DIM,), minval=-lim2, maxval=lim2, dtype=jnp.float32)
        a2 = jax.random.uniform(ks[6], (OUT_DIM,), minval=-lim2, maxval=lim2, dtype=jnp.float32)
        att_b = jax.random.uniform(ks[7], (), minval=-lim2, maxval=lim2, dtype=jnp.float32)
        return {'x': x, 'adj': adj, 'mask': mask, 'W': W, 'b': b, 'a1': a1, 'a2': a2, 'att_b': att_b}
    _L1_gnn_all = _L1_gnn_setup()
    _L1_gnn_in = {k: v for k, v in _L1_gnn_all.items() if k in ('W', 'b', 'a1', 'a2', 'att_b')}
    del _L1_gnn_all

    def _L1_ffn_setup():
        import jax, jax.numpy as jnp
        import numpy as np
        E = 8
        K = 2
        D = 128
        H = 256
        DOUT = 128
        EPS = 1e-05
        key = jax.random.key(seed)
        ks = jax.random.split(key, 9)
        s = 0.02
        return {'x': jax.random.normal(ks[0], (4, 4096, D), jnp.float32), 'gamma': 1.0 + 0.05 * jax.random.normal(ks[1], (D,), jnp.float32), 'beta': 0.05 * jax.random.normal(ks[2], (D,), jnp.float32), 'Wr': 0.01 * jax.random.normal(ks[3], (D, E), jnp.float32), 'br': jnp.zeros((E,), jnp.float32), 'W1': s * jax.random.normal(ks[4], (E, D, H), jnp.float32), 'b1': s * jax.random.normal(ks[5], (E, H), jnp.float32), 'W2': s * jax.random.normal(ks[6], (E, H, DOUT), jnp.float32), 'b2': s * jax.random.normal(ks[7], (E, DOUT), jnp.float32)}
    _L1_ffn_all = _L1_ffn_setup()
    _L1_ffn_in = {k: v for k, v in _L1_ffn_all.items() if k in ('gamma', 'beta', 'Wr', 'br', 'W1', 'b1', 'W2', 'b2')}
    del _L1_ffn_all
    return {'x': x, 'adj': adj, 'nodemask': nodemask, 'L0_gnn_weight': _L0_gnn_in['weight'], 'L0_gnn_bias': _L0_gnn_in['bias'], 'L0_ffn_router_w': _L0_ffn_in['router_w'], 'L0_ffn_router_b': _L0_ffn_in['router_b'], 'L0_ffn_W1': _L0_ffn_in['W1'], 'L0_ffn_b1': _L0_ffn_in['b1'], 'L0_ffn_W2': _L0_ffn_in['W2'], 'L0_ffn_b2': _L0_ffn_in['b2'], 'L1_gnn_W': _L1_gnn_in['W'], 'L1_gnn_b': _L1_gnn_in['b'], 'L1_gnn_a1': _L1_gnn_in['a1'], 'L1_gnn_a2': _L1_gnn_in['a2'], 'L1_gnn_att_b': _L1_gnn_in['att_b'], 'L1_ffn_gamma': _L1_ffn_in['gamma'], 'L1_ffn_beta': _L1_ffn_in['beta'], 'L1_ffn_Wr': _L1_ffn_in['Wr'], 'L1_ffn_br': _L1_ffn_in['br'], 'L1_ffn_W1': _L1_ffn_in['W1'], 'L1_ffn_b1': _L1_ffn_in['b1'], 'L1_ffn_W2': _L1_ffn_in['W2'], 'L1_ffn_b2': _L1_ffn_in['b2']}

def reference(x, adj, nodemask, L0_gnn_weight, L0_gnn_bias, L0_ffn_router_w, L0_ffn_router_b, L0_ffn_W1, L0_ffn_b1, L0_ffn_W2, L0_ffn_b2, L1_gnn_W, L1_gnn_b, L1_gnn_a1, L1_gnn_a2, L1_gnn_att_b, L1_ffn_gamma, L1_ffn_beta, L1_ffn_Wr, L1_ffn_br, L1_ffn_W1, L1_ffn_b1, L1_ffn_W2, L1_ffn_b2):
    import jax
    import jax.numpy as jnp

    def _L0_gnn_ref(x, adj, weight, bias):
        import jax, jax.numpy as jnp
        import numpy as np
        B, N, F_IN, F_OUT = (32, 512, 128, 128)
        EPS = 1e-08
        adj_norm = adj / (jnp.sum(adj, axis=-1, keepdims=True) + EPS)
        h_neigh = jnp.einsum('bnm,bmf->bnf', adj_norm, x)
        h_concat = jnp.concatenate([x, h_neigh], axis=-1)
        h = jnp.einsum('bnk,ko->bno', h_concat, weight) + bias
        return jax.nn.relu(h)

    def _L0_ffn_ref(x, router_w, router_b, W1, b1, W2, b2):
        import jax, jax.numpy as jnp
        import numpy as np
        B, K, D = (256, 16, 128)
        E = 32
        H = int(D * 0.25)
        xf = x.reshape(-1, D)
        logits = xf @ router_w.T + router_b
        idx = jnp.argmax(logits, axis=-1)
        w1t = jnp.take(W1, idx, axis=0)
        h = jnp.einsum('nd,ndh->nh', xf, w1t) + jnp.take(b1, idx, axis=0)
        h = jax.nn.relu(h)
        w2t = jnp.take(W2, idx, axis=0)
        out = jnp.einsum('nh,nhd->nd', h, w2t) + jnp.take(b2, idx, axis=0)
        out = jax.nn.relu(out)
        return out.reshape(x.shape)

    def _L1_gnn_ref(x, adj, mask, W, b, a1, a2, att_b):
        import jax, jax.numpy as jnp
        import numpy as np
        B, N, IN_DIM, OUT_DIM = (8, 1024, 128, 128)
        EDGE_P = 0.02
        MASK_P = 0.9
        h = jnp.einsum('bni,di->bnd', x, W) + b
        s1 = h @ a1
        s2 = h @ a2
        logits = s1[:, :, None] + s2[:, None, :] + att_b
        att = jax.nn.sigmoid(logits) * adj
        att = att * mask[:, :, None] * mask[:, None, :]
        att = att / (jnp.sum(att, axis=-1, keepdims=True) + 1e-08)
        h_new = jnp.einsum('bij,bjd->bid', att, h)
        return h_new * mask[:, :, None]

    def _L1_ffn_ref(x, gamma, beta, Wr, br, W1, b1, W2, b2):
        import jax, jax.numpy as jnp
        import numpy as np
        E = 8
        K = 2
        D = 128
        H = 256
        DOUT = 128
        EPS = 1e-05
        mu = jnp.mean(x, axis=-1, keepdims=True)
        var = jnp.mean(jnp.square(x - mu), axis=-1, keepdims=True)
        xn = (x - mu) * jax.lax.rsqrt(var + EPS) * gamma + beta
        logits = jnp.einsum('bsd,de->bse', xn, Wr) + br
        top_vals, top_idx = jax.lax.top_k(logits, K)
        w = jax.nn.softmax(top_vals, axis=-1)
        w_full = jnp.einsum('bsk,bske->bse', w, jax.nn.one_hot(top_idx, E, dtype=w.dtype))
        y = jnp.zeros(x.shape[:-1] + (DOUT,), x.dtype)
        for e in range(E):
            h = jax.nn.gelu(jnp.einsum('bsd,dh->bsh', xn, W1[e]) + b1[e], approximate=False)
            y_e = jnp.einsum('bsh,hd->bsd', h, W2[e]) + b2[e]
            y = y + y_e * w_full[..., e, None]
        return y
    x = x + _L0_gnn_ref(_layernorm(x, axis=-1), adj, L0_gnn_weight, L0_gnn_bias)
    x = x + _L0_ffn_ref(_layernorm(x, axis=-1), L0_ffn_router_w, L0_ffn_router_b, L0_ffn_W1, L0_ffn_b1, L0_ffn_W2, L0_ffn_b2)
    x = x + _L1_gnn_ref(_layernorm(x, axis=-1), adj, nodemask, L1_gnn_W, L1_gnn_b, L1_gnn_a1, L1_gnn_a2, L1_gnn_att_b)
    x = x + _L1_ffn_ref(_layernorm(x, axis=-1), L1_ffn_gamma, L1_ffn_beta, L1_ffn_Wr, L1_ffn_br, L1_ffn_W1, L1_ffn_b1, L1_ffn_W2, L1_ffn_b2)
    return x

_drawn_inputs = setup_inputs


def setup_inputs(seed=0):
    import zlib

    import numpy as np

    out = dict(_drawn_inputs(seed))
    spreads = {'L0_gnn_bias': (0.0, 0.1), 'L1_ffn_br': (0.0, 0.392)}
    factors = {'L0_ffn_b1': 4.755,
     'L1_gnn_a1': 8.0,
     'L1_gnn_a2': 2.74,
     'L1_ffn_gamma': 8.0,
     'L1_ffn_beta': 8.0,
     'L1_ffn_Wr': 2.944,
     'L1_ffn_b1': 8.0,
     'L1_ffn_b2': 5.025}
    for name, (base, spread) in spreads.items():
        noise = np.random.default_rng([zlib.crc32(name.encode()), seed]).standard_normal(out[name].shape)
        drawn = base * np.exp(spread * noise) if base else spread * noise
        out[name] = jnp.asarray(drawn.astype(out[name].dtype))
    for name, factor in factors.items():
        out[name] = (out[name] * factor).astype(out[name].dtype)
    return out
```

```python
from collections import namedtuple
from contextlib import ExitStack

import numpy as np

import concourse.bass as bass
from concourse import mybir

ALU = mybir.AluOpType
ACT = mybir.ActivationFunctionType
F32 = mybir.dt.float32
F32R = mybir.dt.float32r
BF16 = mybir.dt.bfloat16
AX_X = mybir.AxisListType.X

P = 128
G = 16
NT = 4
N = NT * P
D = 128
E0, H0 = 32, 32
E1, H1 = 8, 256
C0N = E0 * H0 // P
C1N = E1 * H1 // P
LN_EPS = 1e-5
SUM_EPS = 1e-8
OFF = 2.0 ** 120
CW = 256

_COLS = [("wg0", 2 * D), ("w1t", D), ("w1n", D), ("a1a2", D + 2), ("brep", D), ("rw0", E0), ("rw1", E1),
         ("b0", C0N), ("b1", C1N), ("gamma", 1), ("beta", 1), ("attb", 1), ("mask", G * NT),
         ("g0row", D), ("g1row", D), ("rb0", E0), ("rb1", E1), ("rank0", E0), ("rank1", E1),
         ("part", 6), ("b20", D), ("b21", D), ("ident", P)]
COL = {}
_at = 0
for _name, _n in _COLS:
    COL[_name] = (_at, _at + _n)
    _at += _n
SMALL = _at

Graph = namedtuple("Graph", "pair par")


def graph(n):
    return Graph(n // 2, n % 2)


def number(g):
    return g.pair * 2 + g.par


def before(g):
    return Graph(g.pair, 0) if g.par else Graph(g.pair - 1, 1)


class Signal:

    def __init__(self, sem, each=1):
        self.sem, self.each = sem, each

    def after(self, g, k=None):
        k = self.each if k is None else k
        return g.pair * (2 * self.each) + (g.par * self.each + k)


UP_ORDER = [("F", u) for u in range(11)] + [
    ("K", 0), ("K", 1), ("F", 11), ("K", 2), ("K", 3), ("F", 12), ("K", 4), ("K", 5), ("F", 13), ("K", 6), ("K", 7),
    ("F", 14), ("F", 15)]
UP_SLOT = {what: n for n, what in enumerate(UP_ORDER)}


def build(nc, small_d, cbf_d, w0up_d, w1up_d, w0dn_d, w1dn_d, x_d, adj_d, out_d):
    with ExitStack() as ctx:
        def sb(name, shape, dt=F32):
            return ctx.enter_context(nc.sbuf_tensor(name, shape, dt))

        def ps(name, shape, dt=F32):
            return ctx.enter_context(nc.psum_tensor(name, shape, dt))

        def sig(name, each=1):
            return Signal(ctx.enter_context(nc.semaphore(name)), each)

        def sigs(name, n):
            return [sig(f"{name}{i}") for i in range(n)]

        small = sb("small", [P, SMALL])
        cbf = sb("cbf", [P, P + C0N * P + E1 * P], BF16)
        ident_b = cbf[:, 0:P]
        off_w = [cbf[:, P + c * P:P + (c + 1) * P] for c in range(C0N)]
        pick_w = [cbf[:, P + (C0N + e) * P:P + (C0N + e + 1) * P] for e in range(E1)]

        def col(name, a=None, b=None):
            lo, hi = COL[name]
            return small[:, lo + (a or 0):(hi if b is None else lo + b)]

        stage_w = sb("stage_w", [P, E1 * H1])
        wg0 = [sb(f"wg0_{s}", [P, 2 * D], F32R) for s in "hl"]
        wg1 = [sb(f"wg1_{s}", [P, D + 2], F32R) for s in "hl"]
        wv1 = [sb(f"wv1_{s}", [P, P], F32R) for s in "hl"]
        rw0 = [sb(f"rw0_{s}", [P, E0], F32R) for s in "hl"]
        rw1 = [sb(f"rw1_{s}", [P, E1], F32R) for s in "hl"]
        w0up = [sb(f"w0up_{s}", [P, E0 * H0], F32R) for s in "hl"]
        w1up = [sb(f"w1up_{s}", [P, E1 * H1], F32R) for s in "hl"]
        w0dn = sb("w0dn", [P, C0N, D])
        w1dn = sb("w1dn", [P, C1N, D])
        b20 = sb("b20", [P, D], BF16)
        b21 = sb("b21", [P, D], BF16)
        bpart = sb("bpart", [P, 2, 3, D], BF16)
        brest = sb("brest", [P, 2, 2, D])
        bsum = sb("bsum", [P, 2, 2, D])
        half = sb("half", [P, NT])
        e_tile = sb("e_tile", [P, NT])
        score_c = sb("score_c", [P, 1])
        mask2 = sb("mask2", [P, G * NT])
        mcur = sb("mcur", [P, NT])
        m2cur = sb("m2cur", [P, NT])

        xa = sb("xa", [P, 2, NT, D])
        adj = sb("adj", [P, 2, NT, N])
        x1 = sb("x1", [P, NT, D])
        x2 = sb("x2", [P, 2, NT, D])
        x3 = sb("x3", [P, 2, NT, D])
        res = sb("res", [P, 2, NT, D])
        st = sb("st", [P, 4, NT, 6])
        mv = sb("mv", [P, 4, NT, 6])
        ve = sb("ve", [P, 4, NT])
        rstd = sb("rstd", [P, 4, NT])
        xn = [sb(f"xn{i}", [P, NT, D]) for i in range(4)]
        xt_h = [sb(f"xt_h{i}", [P, N], F32R) for i in range(3)]
        xt_l = [sb(f"xt_l{i}", [P, N], F32R) for i in range(3)]
        xg = sb("xg", [P, N])
        xg_h = sb("xg_h", [P, 2, N], F32R)
        xg_l = sb("xg_l", [P, 2, N], F32R)
        ysb = sb("ysb", [P, NT, D + 1])
        zsb = sb("zsb", [P, NT, D])
        usb = sb("usb", [P, NT, D])
        deg = sb("deg", [P, 2, NT])
        lg0 = sb("lg0", [P, NT, E0])
        eq0 = sb("eq0", [P, NT, E0])
        sc0 = sb("sc0", [P, NT, E0])
        m0 = sb("m0", [P, 2, NT])
        sel0 = sb("sel0", [P, NT, P], BF16)
        sel0_t = sb("sel0_t", [P, N], BF16)
        h0 = sb("h0", [P, 2, N])
        yo0 = sb("yo0", [P, N])
        hsb = sb("hsb", [P, NT, D + 1])
        s2c = sb("s2c", [P, NT])
        sgm = sb("sgm", [P, NT, N])
        att = sb("att", [P, NT, N])
        den = sb("den", [P, 4, NT])
        lg1 = sb("lg1", [P, NT, E1])
        r1 = sb("r1", [P, 12, NT, E1])
        q1 = sb("q1", [P, 12, NT])
        w3 = sb("w3", [P, NT, P], BF16)
        w3_t = sb("w3_t", [P, 2, N], BF16)
        gel = sb("gel", [P, 4, N])
        hm = sb("hm", [P, 4, N])
        yo1 = sb("yo1", [P, N])

        up = [ps(f"up{i}", [P, N]) for i in range(2)]
        acc1 = ps("acc1", [P, N])
        wb = ps("wb", [P, N])
        two = ps("two", [P, NT, CW])
        tr = ps("tr", [P, N])
        sp = ps("sp", [P, N])
        acc0 = two[:, 0:2, :].rearrange("p t c -> p (t c)")
        sp_b = sp[:, 0:N // 2].bitcast(BF16)

        small_in, cbf_in, w0up_in, w1up_in, w0dn_in, w1dn_in = (sig(n) for n in (
            "small_in", "cbf_in", "w0up_in", "w1up_in", "w0dn_in", "w1dn_in"))
        x_in, adj_in, res_out = sigs("x_in", 2), sigs("adj_in", 2), sigs("res_out", 2)
        set_dve, set_pool, v_ps, c_ps = sig("set_dve"), sig("set_pool"), sig("v_ps"), sig("c_ps")
        stats, veps, rstd_ok, xn_ok, xt_ps = (sigs(n, 4) for n in (
            "stats", "veps", "rstd_ok", "xn_ok", "xt_ps"))
        moments = [sig(f"moments{i}", 2) for i in range(4)]
        xt_hi, xt_lo = sigs("xt_hi", 4), sigs("xt_lo", 4)
        xg_ok = sig("xg_ok")
        y_ps, y_ok, z_ok = sig("y_ps"), sig("y_ok"), sig("z_ok")
        agg0_ps, deg_ok, u_ok, x1_ok = sig("agg0_ps"), sig("deg_ok", 2), sig("u_ok"), sig("x1_ok")
        lg0_ps, pick0, sel0_ps, sel0_ok = sig("lg0_ps"), sig("pick0", 7), sig("sel0_ps"), sig("sel0_ok")
        up0_ps, h0_ok, dn0_ps, yo0_ok, yot0_ps, x2_ok = (
            sig("up0_ps", C0N), sig("h0_ok", C0N), sig("dn0_ps", C0N), sig("yo0_ok"), sig("yot0_ps"), sig("x2_ok"))
        s1_ps, h_ps, s2_ok, hsb_ok = sig("s1_ps"), sig("h_ps"), sig("s2_ok"), sig("hsb_ok")
        sgm_ok, att_ok, agg1_ps, den_ok, x3_ok = (
            sig("sgm_ok", NT), sig("att_ok", NT), sig("agg1_ps"), sig("den_ok", 4), sig("x3_ok"))
        lg1_ps, pick1, pow1, w3_ps, w3_ok = (
            sig("lg1_ps"), sig("pick1", 21), sig("pow1"), sig("w3_ps"), sig("w3_ok"))
        wb_ps, up1_ps, gel_ok, hm_ok, dn1_ps, yo1_ok, yot1_ps, res_ok = (
            sig("wb_ps", E1), sig("up1_ps", C1N), sig("gel_ok", C1N), sig("hm_ok", C1N), sig("dn1_ps", C1N),
            sig("yo1_ok"), sig("yot1_ps"), sig("res_ok"))
        set_hi, mcur_ok, w3_step = sig("set_hi"), sig("mcur_ok", 2), sig("w3_step", 3)
        SET_DVE, SET_POOL = 9, 4

        block = ctx.enter_context(nc.Block())

        def run(eng, stage):
            stage(None, None, graph(0))
            stage(None, graph(0), graph(1))
            for n in range(3):
                stage(graph(n), graph(n + 1), graph(n + 2))
            with eng.Fori(1, G // 2 - 2) as i:
                stage(Graph(i, 1), Graph(i + 1, 0), Graph(i + 1, 1))
                stage(Graph(i + 1, 0), Graph(i + 1, 1), Graph(i + 2, 0))
            stage(graph(G - 3), graph(G - 2), graph(G - 1))
            stage(graph(G - 2), graph(G - 1), None)
            stage(graph(G - 1), None, None)

        @block.sync
        def _(eng):
            def wait(s, g, k=None):
                eng.wait_ge(s.sem, s.after(g, k))

            def load(g):
                eng.dma_start(xa[:, g.par], x_d[bass.ds(number(g), 1)].rearrange("g p t d -> p (g t) d")
                              ).then_inc(x_in[g.par].sem, 16)
                eng.dma_start(adj[:, g.par], adj_d[bass.ds(number(g), 1)].rearrange("g p t n -> p (g t) n")
                              ).then_inc(adj_in[g.par].sem, 16)

            def store(g):
                wait(res_ok, g)
                eng.dma_start(out_d[bass.ds(number(g), 1)].rearrange("g p t d -> p (g t) d"), res[:, g.par]
                              ).then_inc(res_out[g.par].sem, 16)

            def load_after(g, old):
                wait(att_ok, old)
                load(g)

            eng.dma_start(xa[:, 0], x_d[0]).then_inc(x_in[0].sem, 16)
            eng.dma_start(small[:, :], small_d).then_inc(small_in.sem, 16)
            eng.dma_start(adj[:, 0], adj_d[0]).then_inc(adj_in[0].sem, 16)
            eng.dma_start(cbf[:, :], cbf_d).then_inc(cbf_in.sem, 16)
            eng.dma_start(stage_w[:, 0:E0 * H0], w0up_d).then_inc(w0up_in.sem, 16)
            eng.dma_start(w0dn[:, :, :], w0dn_d).then_inc(w0dn_in.sem, 16)
            load(graph(1))
            eng.dma_start(w1dn[:, :, :], w1dn_d).then_inc(w1dn_in.sem, 16)
            eng.wait_ge(set_dve.sem, SET_DVE - 1)
            eng.dma_start(stage_w[:, :], w1up_d).then_inc(w1up_in.sem, 16)
            load_after(graph(2), graph(0))
            load_after(graph(3), graph(1))
            load_after(graph(4), graph(2))
            store(graph(0))
            load_after(graph(5), graph(3))
            store(graph(1))
            with eng.Fori(1, G // 2 - 2) as i:
                load_after(Graph(i + 2, 0), Graph(i + 1, 0))
                store(Graph(i, 0))
                load_after(Graph(i + 2, 1), Graph(i + 1, 1))
                store(Graph(i, 1))
            for n in range(G - 4, G):
                store(graph(n))
            for par in range(2):
                eng.wait_ge(res_out[par].sem, 16 * (G // 2))

        @block.gpsimd
        def _(eng):
            def wait(s, g, k=None):
                eng.wait_ge(s.sem, s.after(g, k))

            eng.memset(half[:, :], -0.5).then_inc(set_pool.sem, 1)
            eng.memset(e_tile[:, :], float(np.e)).then_inc(set_pool.sem, 1)
            eng.memset(ysb[:, :, D:D + 1], 1.0).then_inc(set_pool.sem, 1)
            eng.memset(hsb[:, :, D:D + 1], 1.0).then_inc(set_pool.sem, 1)
            eng.wait_ge(set_pool.sem, SET_POOL)

            def inv_std(l, g):
                wait(veps[l], g)
                eng.tensor_tensor(rstd[:, l], ve[:, l], half[:, :], ALU.pow).then_inc(rstd_ok[l].sem, 1)

            def stage(f, b, a):
                if a:
                    inv_std(0, a)
                if b:
                    inv_std(3, b)
                if a:
                    inv_std(1, a)
                if b:
                    wait(pick1, b, 11)
                    eng.tensor_tensor(q1[:, 6], e_tile[:, :], q1[:, 5], ALU.pow).then_inc(pow1.sem, 1)
                if a:
                    inv_std(2, a)

            run(eng, stage)

        @block.tensor
        def _(eng):
            mm = nc.tensor.matmul

            def wait(s, g, k=None):
                eng.wait_ge(s.sem, s.after(g, k))

            def three(out, lhs, rhs, start, stop):
                mm(out, lhs[0], rhs[0], start=start, stop=False)
                mm(out, lhs[0], rhs[1], start=False, stop=False)
                return mm(out, lhs[1], rhs[0], start=False, stop=stop)

            eng.wait_ge(small_in.sem, 16)
            mm(two[:, 0, 0:D + 2], col("w1n"), col("a1a2"), start=True, stop=True).then_inc(v_ps.sem, 1)
            mm(two[:, 2, 0:2], col("brep"), col("a1a2", D - 1, D + 1), start=True, stop=True).then_inc(c_ps.sem, 1)
            eng.wait_ge(cbf_in.sem, 16)
            eng.wait_ge(set_dve.sem, SET_DVE - 1)
            eng.wait_ge(set_pool.sem, SET_POOL)

            def turn(l, g, t_free):
                wait(xn_ok[l], g)
                for s, h in t_free:
                    wait(s, h)
                for t in range(NT):
                    last = nc.tensor.transpose(tr[:, t * P:(t + 1) * P], xn[l][:, t, :], col("ident"))
                last.then_inc(xt_ps[l].sem, 1)

            def project0(g, two_free):
                wait(xt_hi[0], g)
                wait(xt_lo[0], g)
                for s, h in two_free:
                    wait(s, h)
                for t in range(NT):
                    x = [xt_h[0][:, t * P:(t + 1) * P], xt_l[0][:, t * P:(t + 1) * P]]
                    last = three(two[:, t, 0:2 * D], x, [wg0[0][:, :], wg0[1][:, :]], True, True)
                last.then_inc(y_ps.sem, 1)

            def gather(g, weights, values, done):
                for t in range(NT):
                    for k in range(NT):
                        last = mm(two[:, t, 0:D + 1], weights[:, k, t * P:(t + 1) * P], values[:, k, :],
                                  start=(k == 0), stop=(k == NT - 1))
                last.then_inc(done.sem, 1)

            def route(g, x, w, n, done):
                for t in range(NT):
                    xs = [x[0][:, t * P:(t + 1) * P], x[1][:, t * P:(t + 1) * P]]
                    last = three(tr[:, t * n:(t + 1) * n], xs, [w[0][:, :], w[1][:, :]], True, True)
                last.then_inc(done.sem, 1)

            def turn_b(src, done):
                for t in range(NT):
                    last = nc.tensor.transpose(sp_b[:, t * P:(t + 1) * P], src[:, t, :], ident_b)
                last.then_inc(done.sem, 1)

            def bank_free(kind, n, f, a):
                s = UP_SLOT[(kind, n)] - 2
                if f is None:
                    if n >= 1:
                        wait(h0_ok, a, n)
                    return
                if s < 0:
                    if number_is(f, 0):
                        return
                    wait(gel_ok, before(f), C1N + s + 1)
                    return
                was, m = UP_ORDER[s]
                if was == "F":
                    wait(gel_ok, f, m + 1)
                elif a:
                    wait(h0_ok, a, m + 1)
                else:
                    m = max(v for k, v in UP_ORDER[:s + 1] if k == "F")
                    wait(gel_ok, f, m + 1)

            def number_is(g, n):
                return not isinstance(g.pair, bass.RuntimeValue) and number(g) == n

            def k_up(c, f, a):
                if c == 0:
                    wait(sel0_ok, a)
                bank_free("K", c, f, a)
                o = up[UP_SLOT[("K", c)] % 2][:, :]
                w = [w0up[0][:, c * P:(c + 1) * P], w0up[1][:, c * P:(c + 1) * P]]
                three(o, w, [xt_h[1][:, :], xt_l[1][:, :]], True, False)
                mm(o, off_w[c], sel0_t[:, :], start=False, stop=True).then_inc(up0_ps.sem, 1)

            def k_down(c, a):
                wait(h0_ok, a, c + 1)
                last = mm(acc0, w0dn[:, c, :], h0[:, c % 2, :], start=(c == 0), stop=False)
                if c == C0N - 1:
                    last = mm(acc0, b20[:, :], sel0_t[:, :], start=False, stop=True)
                last.then_inc(dn0_ps.sem, 1)

            def f_down(u, f):
                wait(hm_ok, f, u + 1)
                last = mm(acc1[:, :], w1dn[:, u, :], hm[:, u % 4, :], start=(u == 0), stop=False)
                if u == C1N - 1:
                    last = mm(acc1[:, :], b21[:, :], w3_t[:, f.par, :], start=False, stop=True)
                last.then_inc(dn1_ps.sem, 1)

            def F(u, f, a, prev):
                if f:
                    if u == 0:
                        wait(xt_hi[3], f)
                        wait(xt_lo[3], f)
                    bank_free("F", u, f, a)
                    w = [w1up[0][:, u * P:(u + 1) * P], w1up[1][:, u * P:(u + 1) * P]]
                    three(up[UP_SLOT[("F", u)] % 2][:, :], w, [xg_h[:, f.par, :], xg_l[:, f.par, :]], True, True
                          ).then_inc(up1_ps.sem, 1)
                    if u % 2 == 1:
                        if u == 1:
                            wait(w3_ok, f)
                            if prev:
                                wait(hm_ok, prev)
                        else:
                            wait(hm_ok, f, u - 1)
                        mm(wb[:, :], pick_w[u // 2], w3_t[:, f.par, :], start=True, stop=True
                           ).then_inc(wb_ps.sem, 1)
                if u < 2:
                    if prev:
                        f_down(C1N - 2 + u, prev)
                elif f:
                    if u == 2 and prev:
                        wait(yo1_ok, prev)
                    f_down(u - 2, f)

            def stage(f, b, a):
                prev = before(f) if f and not number_is(f, 0) else None
                if f and number_is(f, 0):
                    eng.wait_ge(set_dve.sem, SET_DVE)
                    eng.wait_ge(w1dn_in.sem, 16)

                F(0, f, a, prev)
                if b:
                    turn(2, b, [(x2_ok, b)] + ([(pick1, before(b), )] if f else []))
                F(1, f, a, prev)
                if b:
                    wait(xt_hi[2], b)
                    wait(xt_lo[2], b)
                    three(sp[:, :], [wv1[0][:, :], wv1[1][:, :]], [xt_h[2][:, :], xt_l[2][:, :]], True, True
                          ).then_inc(s1_ps.sem, 1)
                    for t in range(NT):
                        x = [xt_h[2][:, t * P:(t + 1) * P], xt_l[2][:, t * P:(t + 1) * P]]
                        last = three(two[:, t, 0:D + 2], x, [wg1[0][:, :], wg1[1][:, :]], True, True)
                    last.then_inc(h_ps.sem, 1)
                if a:
                    turn(0, a, [(xt_lo[2], b)] if b else [])
                F(2, f, a, prev)
                if prev:
                    wait(yo1_ok, prev)
                    wait(xt_lo[0], a) if a else wait(xt_lo[2], b) if b else None
                    for t in range(NT):
                        last = nc.tensor.transpose(tr[:, t * P:(t + 1) * P], yo1[:, t * P:(t + 1) * P], col("ident"))
                    last.then_inc(yot1_ps.sem, 1)
                F(3, f, a, prev)
                if a:
                    project0(a, [(hsb_ok, b), (s2_ok, b)] if b else [])
                F(4, f, a, prev)
                if b:
                    wait(hsb_ok, b)
                    wait(s2_ok, b)
                    if a:
                        wait(z_ok, a)
                        wait(y_ok, a)
                    wait(att_ok, b)
                    gather(b, att, hsb, agg1_ps)
                F(5, f, a, prev)
                if a:
                    wait(y_ok, a)
                    wait(z_ok, a)
                    if b:
                        wait(x3_ok, b)
                    eng.wait_ge(adj_in[a.par].sem, (a.pair + 1) * 16)
                    gather(a, adj[:, a.par], ysb, agg0_ps)
                F(6, f, a, prev)
                F(7, f, a, prev)
                if b:
                    turn(3, b, ([(res_ok, prev)] if prev else []) + ([(xt_lo[0], a)] if a else []))
                F(8, f, a, prev)
                if b:
                    wait(xt_hi[3], b)
                    wait(xt_lo[3], b)
                    route(b, [xg_h[:, b.par, :], xg_l[:, b.par, :]], rw1, E1, lg1_ps)
                if a:
                    xn_wait = [(lg_read1, b)] if b else []
                    for s, h in xn_wait:
                        wait(s, h, 1)
                    turn(1, a, [])
                F(9, f, a, prev)
                if a:
                    wait(xt_hi[1], a)
                    wait(xt_lo[1], a)
                    route(a, [xt_h[1], xt_l[1]], rw0, E0, lg0_ps)
                F(10, f, a, prev)
                if b:
                    wait(pick1, b)
                    turn_b(w3, w3_ps)
                if a:
                    wait(pick0, a)
                    if b:
                        wait(w3_ok, b)
                    turn_b(sel0, sel0_ps)
                    wait(u_ok, a)
                    k_up(0, f, a)
                    k_up(1, f, a)
                F(11, f, a, prev)
                if a:
                    k_down(0, a)
                    k_up(2, f, a)
                    k_down(1, a)
                    k_up(3, f, a)
                F(12, f, a, prev)
                if a:
                    k_down(2, a)
                    k_up(4, f, a)
                    k_down(3, a)
                    k_up(5, f, a)
                F(13, f, a, prev)
                if a:
                    k_down(4, a)
                    k_up(6, f, a)
                    k_down(5, a)
                    k_up(7, f, a)
                F(14, f, a, prev)
                if a:
                    k_down(6, a)
                    k_down(7, a)
                F(15, f, a, prev)
                if a:
                    wait(yo0_ok, a)
                    for t in range(NT):
                        last = nc.tensor.transpose(tr[:, t * P:(t + 1) * P], yo0[:, t * P:(t + 1) * P], col("ident"))
                    last.then_inc(yot0_ps.sem, 1)

            lg_read1 = pick1
            run(eng, stage)
            g = graph(G - 1)
            f_down(C1N - 2, g)
            f_down(C1N - 1, g)
            wait(yo1_ok, g)
            for t in range(NT):
                last = nc.tensor.transpose(tr[:, t * P:(t + 1) * P], yo1[:, t * P:(t + 1) * P], col("ident"))
            last.then_inc(yot1_ps.sem, 1)

        @block.scalar
        def _(eng):
            act = nc.scalar.activation

            def wait(s, g, k=None):
                eng.wait_ge(s.sem, s.after(g, k))

            eng.wait_ge(small_in.sem, 16)

            def first(g):
                return not isinstance(g.pair, bass.RuntimeValue) and number(g) == 0

            def hi(l, g):
                wait(xt_ps[l], g)
                act(xt_h[l][:, :], tr[:, :], ACT.Copy).then_inc(xt_hi[l].sem, 1)

            def F(u, f, prev):
                if f:
                    wait(up1_ps, f, u + 1)
                    if u >= 4:
                        wait(hm_ok, f, u - 3)
                    elif prev:
                        wait(hm_ok, prev, C1N + u - 3)
                    act(gel[:, u % 4, :], up[UP_SLOT[("F", u)] % 2][:, :], ACT.Gelu, bias=col("b1", u, u + 1)
                        ).then_inc(gel_ok.sem, 1)

            def K(c, a):
                wait(up0_ps, a, c + 1)
                if c >= 2:
                    wait(dn0_ps, a, c - 1)
                act(h0[:, c % 2, :], up[UP_SLOT[("K", c)] % 2][:, :], ACT.Relu, bias=col("b0", c, c + 1)
                    ).then_inc(h0_ok.sem, 1)

            def out1(g):
                wait(dn1_ps, g)
                act(yo1[:, :], acc1[:, :], ACT.Copy).then_inc(yo1_ok.sem, 1)

            def stage(f, b, a):
                prev = before(f) if f and not first(f) else None
                F(0, f, prev)
                if b:
                    hi(2, b)
                F(1, f, prev)
                if prev:
                    out1(prev)
                if a:
                    hi(0, a)
                F(2, f, prev)
                if b:
                    wait(s2_ok, b)
                    wait(s1_ps, b)
                    for j in range(NT):
                        act(sgm[:, j, :], sp[:, :], ACT.Sigmoid, bias=s2c[:, j:j + 1]).then_inc(sgm_ok.sem, 1)
                F(3, f, prev)
                if a:
                    wait(y_ps, a)
                    act(ysb[:, :, 0:D], two[:, :, 0:D], ACT.Copy).then_inc(y_ok.sem, 1)
                for u in range(4, 8):
                    F(u, f, prev)
                if b:
                    wait(xg_ok, b)
                    act(xg_h[:, b.par, :], xg[:, :], ACT.Copy).then_inc(xt_hi[3].sem, 1)
                F(8, f, prev)
                if a:
                    hi(1, a)
                F(9, f, prev)
                F(10, f, prev)
                if b:
                    wait(w3_ps, b)
                    act(w3_t[:, b.par, :], sp_b, ACT.Copy).then_inc(w3_ok.sem, 1)
                if a:
                    wait(sel0_ps, a)
                    act(sel0_t[:, :], sp_b, ACT.Copy).then_inc(sel0_ok.sem, 1)
                    K(0, a)
                    K(1, a)
                F(11, f, prev)
                for n in range(3):
                    if a:
                        K(2 + 2 * n, a)
                        K(3 + 2 * n, a)
                    F(12 + n, f, prev)
                F(15, f, prev)
                if a:
                    wait(dn0_ps, a)
                    act(yo0[:, :], acc0, ACT.Relu).then_inc(yo0_ok.sem, 1)

            run(eng, stage)
            out1(graph(G - 1))

        @block.vector
        def _(eng):
            v = nc.vector

            def wait(s, g, k=None):
                eng.wait_ge(s.sem, s.after(g, k))

            def first(g):
                return not isinstance(g.pair, bass.RuntimeValue) and number(g) == 0

            def split(pair, src):
                set_n[0] += 1
                v.tensor_copy(pair[0], src).then_inc(set_hi.sem, 1)
                eng.wait_ge(set_hi.sem, set_n[0])
                return v.tensor_tensor(pair[1], src, pair[0].bitcast(F32), ALU.subtract)

            def part(n, r):
                return col("part", 3 * n + r, 3 * n + r + 1)

            def mask_of(g):
                return col("mask")[:, bass.ds(number(g) * NT, NT)]

            def mask2_of(g):
                return mask2[:, bass.ds(number(g) * NT, NT)]

            set_n = [0]
            v.memset(w3[:, :, :], 0.0)
            v.memset(wg1[0][:, D + 1:D + 2].bitcast(F32), 0.0)
            v.memset(wg1[1][:, D + 1:D + 2].bitcast(F32), 0.0)
            eng.wait_ge(small_in.sem, 16)
            split([wg0[0][:, :], wg0[1][:, :]], col("wg0")).then_inc(set_dve.sem, 1)
            split([wg1[0][:, 0:D], wg1[1][:, 0:D]], col("w1t")).then_inc(set_dve.sem, 1)
            split([rw0[0][:, :], rw0[1][:, :]], col("rw0")).then_inc(set_dve.sem, 1)
            split([rw1[0][:, :], rw1[1][:, :]], col("rw1"))
            eng.wait_ge(v_ps.sem, 1)
            eng.wait_ge(c_ps.sem, 1)
            split([wv1[0][:, :], wv1[1][:, :]], two[:, 0, 0:D]).then_inc(set_dve.sem, 1)
            split([wg1[0][:, D:D + 1], wg1[1][:, D:D + 1]], two[:, 0, D:D + 1]).then_inc(set_dve.sem, 1)
            v.tensor_scalar(score_c[:, :], two[:, 2, 0:1], col("attb"), None, ALU.add).then_inc(set_dve.sem, 1)
            eng.wait_ge(set_dve.sem, 6)
            v.tensor_tensor(score_c[:, :], two[:, 2, 1:2], score_c[:, :], ALU.add)
            v.tensor_tensor(mask2[:, :], col("mask"), col("mask"), ALU.mult)
            for n, name in enumerate(("b20", "b21")):
                def step(ins):
                    set_n[0] += 1
                    ins.then_inc(set_hi.sem, 1)
                    eng.wait_ge(set_hi.sem, set_n[0])
                step(v.tensor_copy(bpart[:, n, 0], col(name)))
                step(v.tensor_tensor(brest[:, n, 0], col(name), bpart[:, n, 0], ALU.subtract))
                step(v.tensor_copy(bpart[:, n, 1], brest[:, n, 0]))
                step(v.tensor_tensor(brest[:, n, 1], brest[:, n, 0], bpart[:, n, 1], ALU.subtract))
                step(v.tensor_copy(bpart[:, n, 2], brest[:, n, 1]))
                step(v.tensor_scalar(bsum[:, n, 0], bpart[:, n, 0], part(n, 0), None, ALU.mult))
                step(v.scalar_tensor_tensor(bsum[:, n, 1], bpart[:, n, 1], part(n, 1), bsum[:, n, 0],
                                            ALU.mult, ALU.add))
                step(v.scalar_tensor_tensor((b20, b21)[n][:, :], bpart[:, n, 2], part(n, 2), bsum[:, n, 1],
                                            ALU.mult, ALU.add))
            eng.wait_ge(w0up_in.sem, 16)
            eng.wait_ge(w0dn_in.sem, 16)
            split([w0up[0][:, :], w0up[1][:, :]], stage_w[:, 0:E0 * H0]).then_inc(set_dve.sem, 1)
            v.memset(deg[:, :, :], 0.0).then_inc(set_dve.sem, 1)

            def norm_a(l, g, x):
                for t in range(NT):
                    last = v.bn_stats(st[:, l, t], x[:, t, :])
                last.then_inc(stats[l].sem, 1)
                wait(stats[l], g)
                even, odd = st[:, l, :, 0:3], st[:, l, :, 3:6]
                v.tensor_tensor(mv[:, l, :, 0:2], even[:, :, 1:3], odd[:, :, 1:3], ALU.add)
                v.tensor_tensor(mv[:, l, :, 2], even[:, :, 1], odd[:, :, 1], ALU.subtract
                                ).then_inc(moments[l].sem, 1)
                wait(moments[l], g, 1)
                v.tensor_scalar(mv[:, l, :, 3], mv[:, l, :, 0], 0.5, None, ALU.mult)
                v.scalar_tensor_tensor(mv[:, l, :, 4], mv[:, l, :, 2], 0.25, mv[:, l, :, 2], ALU.mult, ALU.mult)
                v.tensor_scalar(mv[:, l, :, 5], mv[:, l, :, 1], 1.0 / D, LN_EPS, ALU.mult, ALU.add
                                ).then_inc(moments[l].sem, 1)
                wait(moments[l], g, 2)
                v.tensor_tensor(ve[:, l], mv[:, l, :, 4], mv[:, l, :, 5], ALU.add).then_inc(veps[l].sem, 1)

            def norm_b(l, g, x):
                wait(rstd_ok[l], g)
                for t in range(NT):
                    last = v.tensor_scalar(xn[l][:, t, :], x[:, t, :], mv[:, l, t, 3:4], rstd[:, l, t:t + 1],
                                           ALU.subtract, ALU.mult)
                last.then_inc(xn_ok[l].sem, 1)

            def lo(l, g):
                wait(xt_hi[l], g)
                v.tensor_tensor(xt_l[l][:, :], tr[:, :], xt_h[l][:, :].bitcast(F32), ALU.subtract
                                ).then_inc(xt_lo[l].sem, 1)

            def HM(u, f):
                wait(gel_ok, f, u + 1)
                wait(wb_ps, f, u // 2 + 1)
                if u >= 4:
                    wait(dn1_ps, f, u - 3)
                v.tensor_tensor(hm[:, u % 4, :], gel[:, u % 4, :], wb[:, :], ALU.mult).then_inc(hm_ok.sem, 1)

            def F(u, f, prev):
                if u == 0:
                    if prev:
                        HM(C1N - 1, prev)
                elif f:
                    HM(u - 1, f)

            def spread(ap, n):
                return ap.unsqueeze(2).to_broadcast([P, NT, n])

            def rows(name, n):
                return col(name).unsqueeze(1).to_broadcast([P, NT, n])

            def result(g):
                wait(yot1_ps, g)
                if not first(g) and not (isinstance(g.pair, int) and number(g) < 2):
                    eng.wait_ge(res_out[g.par].sem, g.pair * 16)
                v.tensor_tensor(res[:, g.par], tr[:, :].rearrange("p (t d) -> p t d", t=NT), x3[:, g.par], ALU.add
                                ).then_inc(res_ok.sem, 1)

            def stage(f, b, a):
                prev = before(f) if f and not first(f) else None
                F(0, f, prev)
                if a:
                    eng.wait_ge(x_in[a.par].sem, (a.pair + 1) * 16)
                    norm_a(0, a, xa[:, a.par])
                if b:
                    lo(2, b)
                F(1, f, prev)
                if a:
                    norm_b(0, a, xa[:, a.par])
                if b:
                    wait(h_ps, b)
                    v.tensor_scalar(s2c[:, :], two[:, :, D], score_c[:, 0:1], None, ALU.add).then_inc(s2_ok.sem, 1)
                    v.tensor_tensor(hsb[:, :, 0:D], two[:, :, 0:D], rows("g1row", D), ALU.add
                                    ).then_inc(hsb_ok.sem, 1)
                if a:
                    lo(0, a)
                F(2, f, prev)
                if b:
                    eng.wait_ge(adj_in[b.par].sem, (b.pair + 1) * 16)
                if prev:
                    result(prev)
                if b:
                    for j in range(NT):
                        if j == 2:
                            F(3, f, prev)
                        wait(sgm_ok, b, j + 1)
                        mrow = mcur[:, j:j + 1]
                        if j == 0:
                            v.tensor_copy(mcur[:, :], mask_of(b)).then_inc(mcur_ok.sem, 1)
                            v.tensor_copy(m2cur[:, :], mask2_of(b)).then_inc(mcur_ok.sem, 1)
                            wait(mcur_ok, b)
                        v.scalar_tensor_tensor(att[:, j], sgm[:, j], mrow, adj[:, b.par, j], ALU.mult, ALU.mult
                                               ).then_inc(att_ok.sem, 1)
                else:
                    F(3, f, prev)
                if a:
                    wait(y_ok, a)
                    v.tensor_tensor(zsb[:, :, :], two[:, :, D:2 * D], rows("g0row", D), ALU.add
                                    ).then_inc(z_ok.sem, 1)
                F(4, f, prev)
                F(5, f, prev)
                if b:
                    wait(agg1_ps, b)
                    v.tensor_tensor(den[:, 0], two[:, :, D], mcur[:, :], ALU.mult).then_inc(den_ok.sem, 1)
                    wait(den_ok, b, 1)
                    v.tensor_scalar(den[:, 1], den[:, 0], SUM_EPS, None, ALU.add).then_inc(den_ok.sem, 1)
                    wait(den_ok, b, 2)
                    v.reciprocal(den[:, 2], den[:, 1]).then_inc(den_ok.sem, 1)
                    wait(den_ok, b, 3)
                    v.tensor_tensor(den[:, 3], den[:, 2], m2cur[:, :], ALU.mult).then_inc(den_ok.sem, 1)
                    wait(den_ok, b)
                    for t in range(NT):
                        last = v.scalar_tensor_tensor(x3[:, b.par, t], two[:, t, 0:D], den[:, 3, t:t + 1],
                                                      x2[:, b.par, t], ALU.mult, ALU.add)
                    last.then_inc(x3_ok.sem, 1)
                    wait(x3_ok, b)
                    norm_a(3, b, x3[:, b.par])
                F(6, f, prev)
                if b:
                    norm_b(3, b, x3[:, b.par])
                if a:
                    wait(agg0_ps, a)
                    v.tensor_scalar(deg[:, 0], two[:, :, D], SUM_EPS, None, ALU.add).then_inc(deg_ok.sem, 1)
                    wait(deg_ok, a, 1)
                    v.reciprocal(deg[:, 1], deg[:, 0]).then_inc(deg_ok.sem, 1)
                    wait(deg_ok, a)
                    for t in range(NT):
                        last = v.scalar_tensor_tensor(usb[:, t], two[:, t, 0:D], deg[:, 1, t:t + 1], zsb[:, t],
                                                      ALU.mult, ALU.add)
                    last.then_inc(u_ok.sem, 1)
                    wait(u_ok, a)
                    v.scalar_tensor_tensor(x1[:, :, :], usb[:, :, :], 0.0, xa[:, a.par], ALU.max, ALU.add
                                           ).then_inc(x1_ok.sem, 1)
                    wait(x1_ok, a)
                    norm_a(1, a, x1)
                F(7, f, prev)
                if b:
                    wait(xt_ps[3], b)
                    v.tensor_scalar(xg[:, :], tr[:, :], col("gamma"), col("beta"), ALU.mult, ALU.add
                                    ).then_inc(xg_ok.sem, 1)
                if a:
                    norm_b(1, a, x1)
                if b:
                    wait(xt_hi[3], b)
                    v.tensor_tensor(xg_l[:, b.par, :], xg[:, :], xg_h[:, b.par, :].bitcast(F32), ALU.subtract
                                    ).then_inc(xt_lo[3].sem, 1)
                F(8, f, prev)
                if b:
                    wait(lg1_ps, b)
                    n = [0]

                    def step(ins, k=None):
                        n[0] += 1
                        ins.then_inc(pick1.sem, 1)
                        wait(pick1, b, n[0])
                    R = r1[:, :, :, :]
                    step(v.tensor_tensor(lg1[:, :, :], tr[:, 0:NT * E1].rearrange("p (t e) -> p t e", t=NT),
                                         rows("rb1", E1), ALU.add))
                    step(v.tensor_reduce(q1[:, 0], lg1[:, :, :], AX_X, ALU.max))
                    step(v.tensor_tensor(r1[:, 0], lg1[:, :, :], spread(q1[:, 0], E1), ALU.is_equal))
                    step(v.tensor_tensor(r1[:, 1], r1[:, 0], rows("rank1", E1), ALU.mult))
                    step(v.tensor_reduce(q1[:, 1], r1[:, 1], AX_X, ALU.max))
                    step(v.tensor_tensor(r1[:, 2], r1[:, 1], spread(q1[:, 1], E1), ALU.is_equal))
                    step(v.scalar_tensor_tensor(r1[:, 3], r1[:, 2], -OFF, lg1[:, :, :], ALU.mult, ALU.add))
                    step(v.tensor_reduce(q1[:, 2], r1[:, 3], AX_X, ALU.max))
                    step(v.tensor_tensor(r1[:, 4], r1[:, 3], spread(q1[:, 2], E1), ALU.is_equal))
                    step(v.tensor_tensor(r1[:, 5], r1[:, 4], rows("rank1", E1), ALU.mult))
                    step(v.tensor_tensor(q1[:, 5], q1[:, 2], q1[:, 0], ALU.subtract))
                if a:
                    lo(1, a)
                F(9, f, prev)
                if b:
                    step(v.tensor_reduce(q1[:, 3], r1[:, 5], AX_X, ALU.max))
                    step(v.tensor_tensor(r1[:, 6], r1[:, 5], spread(q1[:, 3], E1), ALU.is_equal))
                    wait(pow1, b)
                    step(v.tensor_scalar(q1[:, 7], q1[:, 6], 1.0, None, ALU.add))
                    step(v.reciprocal(q1[:, 8], q1[:, 7]))
                    step(v.tensor_tensor(r1[:, 7], r1[:, 6], spread(q1[:, 6], E1), ALU.mult))
                    step(v.tensor_tensor(r1[:, 8], r1[:, 7], r1[:, 2], ALU.add))
                    step(v.tensor_tensor(r1[:, 9], r1[:, 8], spread(q1[:, 8], E1), ALU.mult))
                    W = w3[:, :, 0:9 * E1].rearrange("p t (q r e) -> p t q r e", q=3, e=E1)
                    step(v.tensor_copy(W[:, :, 0, 0], r1[:, 9]))
                    step(v.tensor_tensor(r1[:, 10], r1[:, 9], W[:, :, 0, 0], ALU.subtract))
                    v.tensor_copy(W[:, :, 0, 1], r1[:, 10]).then_inc(w3_step.sem, 1)
                    wait(w3_step, b, 1)
                    v.tensor_tensor(r1[:, 11], r1[:, 10], W[:, :, 0, 1], ALU.subtract).then_inc(w3_step.sem, 1)
                    wait(w3_step, b, 2)
                    v.tensor_copy(W[:, :, 0, 2], r1[:, 11]).then_inc(w3_step.sem, 1)
                    wait(w3_step, b, 3)
                    v.tensor_copy(W[:, :, 1], W[:, :, 0])
                    step(v.tensor_copy(W[:, :, 2], W[:, :, 0]))
                if a:
                    wait(lg0_ps, a)
                    n0 = [0]

                    def step0(ins):
                        n0[0] += 1
                        ins.then_inc(pick0.sem, 1)
                        wait(pick0, a, n0[0])
                    step0(v.tensor_tensor(lg0[:, :, :], tr[:, 0:NT * E0].rearrange("p (t e) -> p t e", t=NT),
                                          rows("rb0", E0), ALU.add))
                    step0(v.tensor_reduce(m0[:, 0], lg0[:, :, :], AX_X, ALU.max))
                    step0(v.tensor_tensor(eq0[:, :, :], lg0[:, :, :], spread(m0[:, 0], E0), ALU.is_equal))
                    step0(v.tensor_tensor(sc0[:, :, :], eq0[:, :, :], rows("rank0", E0), ALU.mult))
                    step0(v.tensor_reduce(m0[:, 1], sc0[:, :, :], AX_X, ALU.max))
                    S = sel0[:, :, :].rearrange("p t (r e) -> p t r e", e=E0)
                    v.tensor_tensor(S[:, :, 0], sc0[:, :, :], spread(m0[:, 1], E0), ALU.is_equal)
                    step0(v.tensor_tensor(S[:, :, 3], sc0[:, :, :], spread(m0[:, 1], E0), ALU.not_equal))
                    v.tensor_copy(S[:, :, 1], S[:, :, 0])
                    step0(v.tensor_copy(S[:, :, 2], S[:, :, 0]))
                for u in range(10, 16):
                    F(u, f, prev)
                if a:
                    wait(yot0_ps, a)
                    v.tensor_tensor(x2[:, a.par], tr[:, :].rearrange("p (t d) -> p t d", t=NT), x1[:, :, :], ALU.add
                                    ).then_inc(x2_ok.sem, 1)
                    wait(x2_ok, a)
                    norm_a(2, a, x2[:, a.par])
                    norm_b(2, a, x2[:, a.par])
                if a and not f and not b:
                    eng.wait_ge(w1up_in.sem, 16)
                    split([w1up[0][:, :], w1up[1][:, :]], stage_w[:, :]).then_inc(set_dve.sem, 1)

            run(eng, stage)
            HM(C1N - 1, graph(G - 1))
            result(graph(G - 1))


def kernel(x, adj, nodemask, L0_gnn_weight, L0_gnn_bias, L0_ffn_router_w, L0_ffn_router_b, L0_ffn_W1, L0_ffn_b1,
           L0_ffn_W2, L0_ffn_b2, L1_gnn_W, L1_gnn_b, L1_gnn_a1, L1_gnn_a2, L1_gnn_att_b, L1_ffn_gamma, L1_ffn_beta,
           L1_ffn_Wr, L1_ffn_br, L1_ffn_W1, L1_ffn_b1, L1_ffn_W2, L1_ffn_b2):
    import concourse.bacc as bacc
    import ml_dtypes
    from concourse.bass_utils import run_bass_kernel_spmd

    f = np.float32

    def row(a):
        return np.broadcast_to(np.asarray(a).reshape(1, -1), (P, np.asarray(a).size))

    def padded(a):
        out = np.zeros((P, a.shape[1]), f)
        out[:a.shape[0]] = a
        return out

    top, bottom = np.split(np.asarray(L0_gnn_weight), 2)
    part = np.zeros((P, 6), f)
    for r in range(3):
        part[r * E0:(r + 1) * E0, r] = 1
        part[r * 3 * E1:(r + 1) * 3 * E1, 3 + r] = 1
    pieces = {
        "wg0": np.concatenate([bottom, top], 1),
        "w1t": np.asarray(L1_gnn_W).T, "w1n": np.asarray(L1_gnn_W),
        "a1a2": np.concatenate([np.repeat(np.asarray(L1_gnn_a1)[:, None], P, 1), np.asarray(L1_gnn_a2)[:, None],
                                np.zeros((P, 1), f)], 1),
        "brep": np.repeat(np.asarray(L1_gnn_b)[:, None], P, 1),
        "rw0": np.asarray(L0_ffn_router_w).T, "rw1": np.asarray(L1_ffn_Wr),
        "b0": np.asarray(L0_ffn_b1).reshape(C0N, P).T, "b1": np.asarray(L1_ffn_b1).reshape(C1N, P).T,
        "gamma": np.asarray(L1_ffn_gamma)[:, None], "beta": np.asarray(L1_ffn_beta)[:, None],
        "attb": row(L1_gnn_att_b),
        "mask": np.asarray(nodemask).reshape(G, NT, P).transpose(2, 0, 1).reshape(P, G * NT),
        "g0row": row(L0_gnn_bias), "g1row": row(L1_gnn_b), "rb0": row(L0_ffn_router_b), "rb1": row(L1_ffn_br),
        "rank0": row(np.arange(E0, 0, -1, dtype=f)), "rank1": row(np.arange(E1, 0, -1, dtype=f)),
        "part": part,
        "b20": padded(np.tile(np.asarray(L0_ffn_b2), (3, 1))),
        "b21": padded(np.tile(np.asarray(L1_ffn_b2), (9, 1))),
        "ident": np.eye(P, dtype=f),
    }
    small = np.ascontiguousarray(np.concatenate([pieces[name] for name, _ in _COLS], 1), f)
    cbf = np.zeros((P, P + (C0N + E1) * P), f)
    cbf[:, :P] = np.eye(P)
    for c in range(C0N):
        for j in range(P):
            cbf[3 * E0 + c * (P // H0) + j // H0, P + c * P + j] = -OFF
    for e in range(E1):
        cbf[[e, E1 + e, 2 * E1 + e], P + (C0N + e) * P:P + (C0N + e + 1) * P] = 1
    arrays = {
        "small": small,
        "cbf": cbf.astype(ml_dtypes.bfloat16),
        "w0up": np.asarray(L0_ffn_W1).transpose(1, 0, 2).reshape(D, E0 * H0),
        "w1up": np.asarray(L1_ffn_W1).transpose(1, 0, 2).reshape(D, E1 * H1),
        "w0dn": np.asarray(L0_ffn_W2).reshape(C0N, P, D).transpose(1, 0, 2),
        "w1dn": np.asarray(L1_ffn_W2).reshape(C1N, P, D).transpose(1, 0, 2),
        "x": np.asarray(x).reshape(G, NT, P, D).transpose(0, 2, 1, 3),
        "adj": np.asarray(adj).transpose(0, 2, 1).reshape(G, NT, P, N).transpose(0, 2, 1, 3),
    }
    arrays = {f"in_{name}": np.ascontiguousarray(a) for name, a in arrays.items()}
    nc = bacc.Bacc("TRN2", target_bir_lowering=False, num_devices=1)
    args = [nc.dram_tensor(name, a.shape, mybir.dt.from_np(a.dtype), kind="ExternalInput").ap()
            for name, a in arrays.items()]
    out = nc.dram_tensor("out", (G, P, NT, D), F32, kind="ExternalOutput").ap()
    build(nc, *args, out)
    r = run_bass_kernel_spmd(nc, [arrays], core_ids=[0])
    return r.results[0]["out"].transpose(0, 2, 1, 3).reshape(G, N, D)
```

```python
from collections import namedtuple
from contextlib import ExitStack

import numpy as np

import concourse.bass as bass
from concourse import mybir

ALU = mybir.AluOpType
ACT = mybir.ActivationFunctionType
F32 = mybir.dt.float32
F32R = mybir.dt.float32r
BF16 = mybir.dt.bfloat16
AX_X = mybir.AxisListType.X

P = 128
G = 16
NT = 4
N = NT * P
D = 128
E0, H0 = 32, 32
E1, H1 = 8, 256
C0N = E0 * H0 // P
C1N = E1 * H1 // P
LN_EPS = 1e-5
SUM_EPS = 1e-8
OFF = 2.0 ** 120
CW = 256

_COLS = [("wg0", 2 * D), ("w1t", D), ("w1n", D), ("a1a2", D + 2), ("brep", D), ("rw0", E0), ("rw1", E1),
         ("b0", C0N), ("b1", C1N), ("gamma", 1), ("beta", 1), ("attb", 1), ("mask", G * NT),
         ("g0row", D), ("g1row", D), ("rb0", E0), ("rb1", E1), ("rank0", E0), ("rank1", E1),
         ("part", 6), ("b20", D), ("b21", D), ("ident", P)]
COL = {}
_at = 0
for _name, _n in _COLS:
    COL[_name] = (_at, _at + _n)
    _at += _n
SMALL = _at

Graph = namedtuple("Graph", "pair par")


def graph(n):
    return Graph(n // 2, n % 2)


def number(g):
    return g.pair * 2 + g.par


def before(g):
    return Graph(g.pair, 0) if g.par else Graph(g.pair - 1, 1)


class Signal:

    def __init__(self, sem, each=1):
        self.sem, self.each = sem, each

    def after(self, g, k=None):
        k = self.each if k is None else k
        return g.pair * (2 * self.each) + (g.par * self.each + k)


UNITS = [("F", n // 2) if n % 2 == 0 else ("K", n // 2) for n in range(2 * C0N)] + [
    ("F", u) for u in range(C0N, C1N)]
SLOT = {what: n for n, what in enumerate(UNITS)}


def build(nc, small_d, cbf_d, w0up_d, w1up_d, w0dn_d, w1dn_d, x_d, adj_d, out_d):
    with ExitStack() as ctx:
        def sb(name, shape, dt=F32):
            return ctx.enter_context(nc.sbuf_tensor(name, shape, dt))

        def ps(name, shape, dt=F32):
            return ctx.enter_context(nc.psum_tensor(name, shape, dt))

        def sig(name, each=1):
            return Signal(ctx.enter_context(nc.semaphore(name)), each)

        def sigs(name, n):
            return [sig(f"{name}{i}") for i in range(n)]

        small = sb("small", [P, SMALL])
        cbf = sb("cbf", [P, P + C0N * P + E1 * P], BF16)
        ident_b = cbf[:, 0:P]
        off_w = [cbf[:, P + c * P:P + (c + 1) * P] for c in range(C0N)]
        pick_w = [cbf[:, P + (C0N + e) * P:P + (C0N + e + 1) * P] for e in range(E1)]

        def col(name, a=None, b=None):
            lo, hi = COL[name]
            return small[:, lo + (a or 0):(hi if b is None else lo + b)]

        stage_w = sb("stage_w", [P, E1 * H1])
        wg0 = [sb(f"wg0_{s}", [P, 2 * D], F32R) for s in "hl"]
        wg1 = [sb(f"wg1_{s}", [P, D + 2], F32R) for s in "hl"]
        wv1 = [sb(f"wv1_{s}", [P, P], F32R) for s in "hl"]
        rw0 = [sb(f"rw0_{s}", [P, E0], F32R) for s in "hl"]
        rw1 = [sb(f"rw1_{s}", [P, E1], F32R) for s in "hl"]
        w0up = [sb(f"w0up_{s}", [P, E0 * H0], F32R) for s in "hl"]
        w1up = [sb(f"w1up_{s}", [P, E1 * H1], F32R) for s in "hl"]
        w0dn = sb("w0dn", [P, C0N, D])
        w1dn = sb("w1dn", [P, C1N, D])
        b20 = sb("b20", [P, D], BF16)
        b21 = sb("b21", [P, D], BF16)
        bpart = sb("bpart", [P, 2, 3, D], BF16)
        brest = sb("brest", [P, 2, 2, D])
        bsum = sb("bsum", [P, 2, 2, D])
        half = sb("half", [P, NT])
        e_tile = sb("e_tile", [P, NT])
        score_c = sb("score_c", [P, 1])
        mask2 = sb("mask2", [P, G * NT])
        mcur = sb("mcur", [P, NT])
        m2cur = sb("m2cur", [P, NT])

        xa = sb("xa", [P, 2, NT, D])
        adj = sb("adj", [P, 2, NT, N])
        x1 = sb("x1", [P, 2, NT, D])
        x2 = sb("x2", [P, 2, NT, D])
        x3 = sb("x3", [P, 2, NT, D])
        res = sb("res", [P, 2, NT, D])
        st = sb("st", [P, 4, NT, 6])
        mv = sb("mv", [P, 4, NT, 6])
        ve = sb("ve", [P, 4, NT])
        rstd = sb("rstd", [P, 4, NT])
        xn = [sb(f"xn{i}", [P, NT, D]) for i in range(4)]
        xt_h = [sb(f"xt_h{i}", [P, N], F32R) for i in range(3)]
        xt_l = [sb(f"xt_l{i}", [P, N], F32R) for i in range(3)]
        xg = sb("xg", [P, N])
        xg_h = sb("xg_h", [P, 2, N], F32R)
        xg_l = sb("xg_l", [P, 2, N], F32R)
        ysb = sb("ysb", [P, NT, D + 1])
        zsb = sb("zsb", [P, NT, D])
        usb = sb("usb", [P, NT, D])
        deg = sb("deg", [P, 2, NT])
        lg0 = sb("lg0", [P, NT, E0])
        eq0 = sb("eq0", [P, NT, E0])
        sc0 = sb("sc0", [P, NT, E0])
        m0 = sb("m0", [P, 2, NT])
        sel0 = sb("sel0", [P, NT, P], BF16)
        sel0_t = sb("sel0_t", [P, N], BF16)
        h0 = sb("h0", [P, 2, N])
        yo0 = sb("yo0", [P, N])
        hsb = sb("hsb", [P, NT, D + 1])
        s2c = sb("s2c", [P, NT])
        sgm = sb("sgm", [P, NT, N])
        att = sb("att", [P, NT, N])
        den = sb("den", [P, 4, NT])
        lg1 = sb("lg1", [P, NT, E1])
        r1 = sb("r1", [P, 12, NT, E1])
        q1 = sb("q1", [P, 12, NT])
        w3 = sb("w3", [P, NT, P], BF16)
        w3_t = sb("w3_t", [P, 2, N], BF16)
        gel = sb("gel", [P, 4, N])
        hm = sb("hm", [P, 4, N])
        yo1 = sb("yo1", [P, N])

        up = [ps(f"up{i}", [P, N]) for i in range(2)]
        acc1 = ps("acc1", [P, N])
        wb = ps("wb", [P, N])
        two = ps("two", [P, NT, CW])
        tr = ps("tr", [P, N])
        acc0 = ps("acc0", [P, N])
        tr_b = tr[:, 0:N // 2].bitcast(BF16)

        small_in, cbf_in, w0up_in, w1up_in, w0dn_in, w1dn_in = (sig(n) for n in (
            "small_in", "cbf_in", "w0up_in", "w1up_in", "w0dn_in", "w1dn_in"))
        x_in, adj_in, res_out = sigs("x_in", 2), sigs("adj_in", 2), sigs("res_out", 2)
        set0_ok, set1_ok, set2_ok, set_pool, v_ps, c_ps = sig("set0_ok"), sig("set1_ok"), sig("set2_ok"), sig("set_pool"), sig("v_ps"), sig("c_ps")
        stats, veps, rstd_ok, xn_ok, xt_ps = (sigs(n, 4) for n in (
            "stats", "veps", "rstd_ok", "xn_ok", "xt_ps"))
        moments = [sig(f"moments{i}", 2) for i in range(4)]
        xt_hi, xt_lo = sigs("xt_hi", 4), sigs("xt_lo", 4)
        xg_ok = sig("xg_ok")
        y_ps, z_ok = sig("y_ps"), sig("z_ok")
        agg0_ps, deg_ok, u_ok, x1_ok = sig("agg0_ps"), sig("deg_ok", 2), sig("u_ok"), sig("x1_ok")
        lg0_ps, pick0, sel0_ps, sel0_ok = sig("lg0_ps"), sig("pick0", 7), sig("sel0_ps"), sig("sel0_ok")
        up0_ps, h0_ok, dn0_ps, yo0_ok, yot0_ps, x2_ok = (
            sig("up0_ps", C0N), sig("h0_ok", C0N), sig("dn0_ps", C0N), sig("yo0_ok"), sig("yot0_ps"), sig("x2_ok"))
        s1_ps, h_ps, s2_ok, hsb_ok = sig("s1_ps"), sig("h_ps"), sig("s2_ok"), sig("hsb_ok")
        sgm_ok, att_ok, agg1_ps, den_ok, x3_ok = (
            sig("sgm_ok", NT), sig("att_ok", NT), sig("agg1_ps"), sig("den_ok", 4), sig("x3_ok"))
        lg1_ps, pick1, pow1, w3_ps, w3_ok = (
            sig("lg1_ps"), sig("pick1", 21), sig("pow1"), sig("w3_ps"), sig("w3_ok"))
        wb_ps, up1_ps, gel_ok, hm_ok, dn1_ps, yo1_ok, yot1_ps, res_ok = (
            sig("wb_ps", E1), sig("up1_ps", C1N), sig("gel_ok", C1N), sig("hm_ok", C1N), sig("dn1_ps", C1N),
            sig("yo1_ok"), sig("yot1_ps"), sig("res_ok"))
        set_step, mcur_ok, w3_step = sig("set_hi"), sig("mcur_ok", 2), sig("w3_step", 3)
        SET_POOL = 4

        block = ctx.enter_context(nc.Block())

        def run(stage, eng):
            def at(f):
                stage(*[graph(n) if 0 <= n < G else None for n in range(f, f + 5)])

            for f in range(-4, 3):
                at(f)
            with eng.Fori(1, 1 + (G - 8) // 2) as i:
                stage(Graph(i, 1), Graph(i + 1, 0), Graph(i + 1, 1), Graph(i + 2, 0), Graph(i + 2, 1))
                stage(Graph(i + 1, 0), Graph(i + 1, 1), Graph(i + 2, 0), Graph(i + 2, 1), Graph(i + 3, 0))
            for f in range(G - 5, G):
                at(f)

        @block.sync
        def _(eng):
            def wait(s, g, k=None):
                eng.wait_ge(s.sem, s.after(g, k))

            def load_x(g):
                eng.dma_start(xa[:, g.par], x_d[bass.ds(number(g), 1)].rearrange("g p t d -> p (g t) d")
                              ).then_inc(x_in[g.par].sem, 16)

            def load_adj(g, j):
                eng.dma_start(adj[:, g.par, j], adj_d[bass.ds(number(g), 1), :, j].rearrange("g p n -> p (g n)")
                              ).then_inc(adj_in[g.par].sem, 16)

            def store(g):
                wait(res_ok, g)
                eng.dma_start(out_d[bass.ds(number(g), 1)].rearrange("g p t d -> p (g t) d"), res[:, g.par]
                              ).then_inc(res_out[g.par].sem, 16)

            load_x(graph(0))
            eng.dma_start(small[:, :], small_d).then_inc(small_in.sem, 16)
            for j in range(NT):
                load_adj(graph(0), j)
            load_x(graph(1))
            eng.dma_start(cbf[:, :], cbf_d).then_inc(cbf_in.sem, 16)
            eng.dma_start(stage_w[:, 0:E0 * H0], w0up_d).then_inc(w0up_in.sem, 16)
            eng.dma_start(w0dn[:, :, :], w0dn_d).then_inc(w0dn_in.sem, 16)
            for j in range(NT):
                load_adj(graph(1), j)
            eng.wait_ge(set1_ok.sem, 1)
            eng.dma_start(stage_w[:, :], w1up_d).then_inc(w1up_in.sem, 16)
            eng.dma_start(w1dn[:, :, :], w1dn_d).then_inc(w1dn_in.sem, 16)

            def stage(f, b, k, a, nx):
                if b and a:
                    for j in range(NT):
                        wait(att_ok, b, j + 1)
                        load_adj(a, j)
                if a and number_after(a, 2) is not None:
                    wait(x1_ok, a)
                    load_x(number_after(a, 2))
                if f and not (isinstance(f.pair, int) and number(f) == 0):
                    store(before(f))

            def number_after(g, n):
                if isinstance(g.pair, int) and number(g) + n >= G:
                    return None
                return Graph(g.pair + n // 2, g.par)

            run(stage, eng)
            store(graph(G - 1))
            for par in range(2):
                eng.wait_ge(res_out[par].sem, 16 * (G // 2))

        @block.gpsimd
        def _(eng):
            def wait(s, g, k=None):
                eng.wait_ge(s.sem, s.after(g, k))

            eng.memset(half[:, :], -0.5).then_inc(set_pool.sem, 1)
            eng.memset(e_tile[:, :], float(np.e)).then_inc(set_pool.sem, 1)
            eng.memset(ysb[:, :, D:D + 1], 1.0).then_inc(set_pool.sem, 1)
            eng.memset(hsb[:, :, D:D + 1], 1.0).then_inc(set_pool.sem, 1)
            eng.wait_ge(set_pool.sem, SET_POOL)

            def inv_std(l, g):
                wait(veps[l], g)
                eng.tensor_tensor(rstd[:, l], ve[:, l], half[:, :], ALU.pow).then_inc(rstd_ok[l].sem, 1)

            def stage(f, b, k, a, nx):
                if b:
                    inv_std(3, b)
                if a:
                    inv_std(1, a)
                if b:
                    wait(pick1, b, 11)
                    eng.tensor_tensor(q1[:, 6], e_tile[:, :], q1[:, 5], ALU.pow).then_inc(pow1.sem, 1)
                if k:
                    inv_std(2, k)
                if nx:
                    inv_std(0, nx)

            run(stage, eng)

        @block.tensor
        def _(eng):
            mm = nc.tensor.matmul

            def wait(s, g, k=None):
                eng.wait_ge(s.sem, s.after(g, k))

            def three(out, lhs, rhs, start, stop):
                mm(out, lhs[0], rhs[0], start=start, stop=False)
                mm(out, lhs[0], rhs[1], start=False, stop=False)
                return mm(out, lhs[1], rhs[0], start=False, stop=stop)

            eng.wait_ge(small_in.sem, 16)
            mm(two[:, 0, 0:D + 2], col("w1n"), col("a1a2"), start=True, stop=True).then_inc(v_ps.sem, 1)
            mm(two[:, 2, 0:2], col("brep"), col("a1a2", D - 1, D + 1), start=True, stop=True).then_inc(c_ps.sem, 1)
            eng.wait_ge(cbf_in.sem, 16)
            eng.wait_ge(set0_ok.sem, 1)
            eng.wait_ge(set_pool.sem, SET_POOL)

            def first(g):
                return isinstance(g.pair, int) and number(g) == 0

            def turn(l, g, t_free):
                wait(xn_ok[l], g)
                for s, h in t_free:
                    wait(s, h)
                for t in range(NT):
                    last = nc.tensor.transpose(tr[:, t * P:(t + 1) * P], xn[l][:, t, :], col("ident"))
                last.then_inc(xt_ps[l].sem, 1)

            def project0(g, two_free):
                wait(xt_hi[0], g)
                wait(xt_lo[0], g)
                for s, h in two_free:
                    wait(s, h)
                for t in range(NT):
                    x = [xt_h[0][:, t * P:(t + 1) * P], xt_l[0][:, t * P:(t + 1) * P]]
                    last = three(two[:, t, 0:2 * D], x, [wg0[0][:, :], wg0[1][:, :]], True, True)
                last.then_inc(y_ps.sem, 1)

            def gather(g, weights, values, done):
                for t in range(NT):
                    for k in range(NT):
                        last = mm(two[:, t, 0:D + 1], weights[:, k, t * P:(t + 1) * P], values[:, k, :],
                                  start=(k == 0), stop=(k == NT - 1))
                last.then_inc(done.sem, 1)

            def route(g, x, w, n, done):
                for t in range(NT):
                    xs = [x[0][:, t * P:(t + 1) * P], x[1][:, t * P:(t + 1) * P]]
                    last = three(tr[:, t * n:(t + 1) * n], xs, [w[0][:, :], w[1][:, :]], True, True)
                last.then_inc(done.sem, 1)

            def turn_b(src, done):
                for t in range(NT):
                    last = nc.tensor.transpose(tr_b[:, t * P:(t + 1) * P], src[:, t, :], ident_b)
                last.then_inc(done.sem, 1)

            def back(g, src, done):
                for t in range(NT):
                    last = nc.tensor.transpose(tr[:, t * P:(t + 1) * P], src[:, t * P:(t + 1) * P], col("ident"))
                last.then_inc(done.sem, 1)

            def up_free(n, f, k):
                if n < 2:
                    if f and not first(f):
                        wait(gel_ok, before(f), C1N + n - 1)
                elif UNITS[n - 2][0] == "F":
                    if f:
                        wait(gel_ok, f, UNITS[n - 2][1] + 1)
                elif k:
                    wait(h0_ok, k, UNITS[n - 2][1] + 1)

            def k_down(c, k):
                wait(h0_ok, k, c + 1)
                last = mm(acc0[:, :], w0dn[:, c, :], h0[:, c % 2, :], start=(c == 0), stop=False)
                if c == C0N - 1:
                    last = mm(acc0[:, :], b20[:, :], sel0_t[:, :], start=False, stop=True)
                last.then_inc(dn0_ps.sem, 1)

            def f_down(u, f):
                wait(hm_ok, f, u + 1)
                last = mm(acc1[:, :], w1dn[:, u, :], hm[:, u % 4, :], start=(u == 0), stop=False)
                if u == C1N - 1:
                    last = mm(acc1[:, :], b21[:, :], w3_t[:, f.par, :], start=False, stop=True)
                last.then_inc(dn1_ps.sem, 1)

            def unit(n, f, k):
                kind, u = UNITS[n]
                if kind == "K":
                    if k:
                        if u == 0:
                            wait(sel0_ok, k)
                        up_free(n, f, k)
                        w = [w0up[0][:, u * P:(u + 1) * P], w0up[1][:, u * P:(u + 1) * P]]
                        three(up[n % 2][:, :], w, [xt_h[1][:, :], xt_l[1][:, :]], True, False)
                        mm(up[n % 2][:, :], off_w[u], sel0_t[:, :], start=False, stop=True).then_inc(up0_ps.sem, 1)
                        if u >= 1:
                            k_down(u - 1, k)
                    return
                prev = before(f) if f and not first(f) else None
                if f:
                    if u == 0:
                        wait(xt_hi[3], f)
                        wait(xt_lo[3], f)
                    up_free(n, f, k)
                    w = [w1up[0][:, u * P:(u + 1) * P], w1up[1][:, u * P:(u + 1) * P]]
                    three(up[n % 2][:, :], w, [xg_h[:, f.par, :], xg_l[:, f.par, :]], True, True
                          ).then_inc(up1_ps.sem, 1)
                    if u % 2 == 1:
                        if u == 1:
                            wait(w3_ok, f)
                            if prev:
                                wait(hm_ok, prev)
                        else:
                            wait(hm_ok, f, u - 1)
                        mm(wb[:, :], pick_w[u // 2], w3_t[:, f.par, :], start=True, stop=True
                           ).then_inc(wb_ps.sem, 1)
                if u < 2:
                    if prev:
                        f_down(C1N - 2 + u, prev)
                elif f:
                    if u == 2 and prev:
                        wait(yo1_ok, prev)
                    f_down(u - 2, f)

            def stage(f, b, k, a, nx):
                prev = before(f) if f and not first(f) else None
                if k and first(k):
                    eng.wait_ge(set1_ok.sem, 1)
                    eng.wait_ge(w0dn_in.sem, 16)
                if f and first(f):
                    eng.wait_ge(set2_ok.sem, 1)
                    eng.wait_ge(w1dn_in.sem, 16)
                unit(0, f, k)
                if b:
                    turn(2, b, [(sel0_ok, k)] if k else [])
                unit(1, f, k)
                if a:
                    turn(0, a, [(xt_lo[2], b)] if b else [(sel0_ok, k)] if k else [])
                unit(2, f, k)
                if b:
                    wait(xt_hi[2], b)
                    wait(xt_lo[2], b)
                    if a:
                        wait(xt_lo[0], a)
                    three(tr[:, :], [wv1[0][:, :], wv1[1][:, :]], [xt_h[2][:, :], xt_l[2][:, :]], True, True
                          ).then_inc(s1_ps.sem, 1)
                    for t in range(NT):
                        x = [xt_h[2][:, t * P:(t + 1) * P], xt_l[2][:, t * P:(t + 1) * P]]
                        last = three(two[:, t, 0:D + 2], x, [wg1[0][:, :], wg1[1][:, :]], True, True)
                    last.then_inc(h_ps.sem, 1)
                unit(3, f, k)
                unit(4, f, k)
                if a:
                    project0(a, [(hsb_ok, b), (s2_ok, b)] if b else [])
                unit(5, f, k)
                if prev:
                    wait(yo1_ok, prev)
                    if b:
                        wait(sgm_ok, b)
                    back(prev, yo1, yot1_ps)
                unit(6, f, k)
                unit(7, f, k)
                if b:
                    wait(hsb_ok, b)
                    wait(s2_ok, b)
                    if a:
                        wait(z_ok, a)
                    wait(att_ok, b)
                    gather(b, att, hsb, agg1_ps)
                unit(8, f, k)
                unit(9, f, k)
                unit(10, f, k)
                if a:
                    wait(z_ok, a)
                    if b:
                        wait(x3_ok, b)
                    eng.wait_ge(adj_in[a.par].sem, (a.pair + 1) * (16 * NT))
                    gather(a, adj[:, a.par], ysb, agg0_ps)
                unit(11, f, k)
                unit(12, f, k)
                if b:
                    turn(3, b, [(res_ok, prev)] if prev else [])
                unit(13, f, k)
                unit(14, f, k)
                if b:
                    wait(xt_hi[3], b)
                    wait(xt_lo[3], b)
                    route(b, [xg_h[:, b.par, :], xg_l[:, b.par, :]], rw1, E1, lg1_ps)
                unit(15, f, k)
                if a:
                    if b:
                        wait(pick1, b, 1)
                    turn(1, a, [])
                unit(16, f, k)
                unit(17, f, k)
                if k:
                    k_down(C0N - 1, k)
                if a:
                    wait(xt_hi[1], a)
                    wait(xt_lo[1], a)
                    route(a, [xt_h[1], xt_l[1]], rw0, E0, lg0_ps)
                unit(18, f, k)
                unit(19, f, k)
                if b:
                    wait(pick1, b)
                    if a:
                        wait(pick0, a, 1)
                    turn_b(w3, w3_ps)
                unit(20, f, k)
                if k:
                    wait(yo0_ok, k)
                    if b:
                        wait(w3_ok, b)
                    if a:
                        wait(pick0, a, 1)
                    back(k, yo0, yot0_ps)
                unit(21, f, k)
                unit(22, f, k)
                if a:
                    wait(pick0, a)
                    if k:
                        wait(x2_ok, k)
                    turn_b(sel0, sel0_ps)
                unit(23, f, k)

            run(stage, eng)
            g = graph(G - 1)
            f_down(C1N - 2, g)
            f_down(C1N - 1, g)
            wait(yo1_ok, g)
            back(g, yo1, yot1_ps)

        @block.scalar
        def _(eng):
            act = nc.scalar.activation

            def wait(s, g, k=None):
                eng.wait_ge(s.sem, s.after(g, k))

            eng.wait_ge(small_in.sem, 16)

            def first(g):
                return isinstance(g.pair, int) and number(g) == 0

            def hi(l, g):
                wait(xt_ps[l], g)
                act(xt_h[l][:, :], tr[:, :], ACT.Copy).then_inc(xt_hi[l].sem, 1)

            def unit(n, f, k):
                kind, u = UNITS[n]
                if kind == "K":
                    if k:
                        wait(up0_ps, k, u + 1)
                        if u >= 2:
                            wait(dn0_ps, k, u - 1)
                        act(h0[:, u % 2, :], up[n % 2][:, :], ACT.Relu, bias=col("b0", u, u + 1)
                            ).then_inc(h0_ok.sem, 1)
                elif f:
                    wait(up1_ps, f, u + 1)
                    if u >= 4:
                        wait(hm_ok, f, u - 3)
                    elif not first(f):
                        wait(hm_ok, before(f), C1N + u - 3)
                    act(gel[:, u % 4, :], up[n % 2][:, :], ACT.Gelu, bias=col("b1", u, u + 1)
                        ).then_inc(gel_ok.sem, 1)

            def out1(g):
                wait(dn1_ps, g)
                act(yo1[:, :], acc1[:, :], ACT.Copy).then_inc(yo1_ok.sem, 1)

            def stage(f, b, k, a, nx):
                unit(0, f, k)
                if b:
                    hi(2, b)
                unit(1, f, k)
                if a:
                    hi(0, a)
                unit(2, f, k)
                if f and not first(f):
                    out1(before(f))
                unit(3, f, k)
                if b:
                    wait(s2_ok, b)
                    wait(s1_ps, b)
                    for j in range(NT):
                        act(sgm[:, j, :], tr[:, :], ACT.Sigmoid, bias=s2c[:, j:j + 1]).then_inc(sgm_ok.sem, 1)
                for n in range(4, 14):
                    unit(n, f, k)
                if b:
                    wait(xg_ok, b)
                    act(xg_h[:, b.par, :], xg[:, :], ACT.Copy).then_inc(xt_hi[3].sem, 1)
                unit(14, f, k)
                unit(15, f, k)
                if a:
                    hi(1, a)
                unit(16, f, k)
                unit(17, f, k)
                unit(18, f, k)
                if k:
                    wait(dn0_ps, k)
                    act(yo0[:, :], acc0[:, :], ACT.Relu).then_inc(yo0_ok.sem, 1)
                unit(19, f, k)
                if b:
                    wait(w3_ps, b)
                    act(w3_t[:, b.par, :], tr_b, ACT.Copy).then_inc(w3_ok.sem, 1)
                unit(20, f, k)
                unit(21, f, k)
                unit(22, f, k)
                if a:
                    wait(sel0_ps, a)
                    act(sel0_t[:, :], tr_b, ACT.Copy).then_inc(sel0_ok.sem, 1)
                unit(23, f, k)

            run(stage, eng)
            out1(graph(G - 1))

        @block.vector
        def _(eng):
            v = nc.vector

            def wait(s, g, k=None):
                eng.wait_ge(s.sem, s.after(g, k))

            def first(g):
                return isinstance(g.pair, int) and number(g) == 0

            step_n = [0]

            def step(ins):
                step_n[0] += 1
                ins.then_inc(set_step.sem, 1)
                eng.wait_ge(set_step.sem, step_n[0])

            def split(pair, src):
                step(v.tensor_copy(pair[0], src))
                step(v.tensor_tensor(pair[1], src, pair[0].bitcast(F32), ALU.subtract))

            def bias_parts(n, name, out):
                def rows_of(r):
                    return col("part", 3 * n + r, 3 * n + r + 1)

                step(v.tensor_copy(bpart[:, n, 0], col(name)))
                step(v.tensor_tensor(brest[:, n, 0], col(name), bpart[:, n, 0], ALU.subtract))
                step(v.tensor_copy(bpart[:, n, 1], brest[:, n, 0]))
                step(v.tensor_tensor(brest[:, n, 1], brest[:, n, 0], bpart[:, n, 1], ALU.subtract))
                step(v.tensor_copy(bpart[:, n, 2], brest[:, n, 1]))
                step(v.tensor_scalar(bsum[:, n, 0], bpart[:, n, 0], rows_of(0), None, ALU.mult))
                step(v.scalar_tensor_tensor(bsum[:, n, 1], bpart[:, n, 1], rows_of(1), bsum[:, n, 0],
                                            ALU.mult, ALU.add))
                step(v.scalar_tensor_tensor(out, bpart[:, n, 2], rows_of(2), bsum[:, n, 1], ALU.mult, ALU.add))

            def mask_of(g, m):
                return m[:, bass.ds(number(g) * NT, NT)]

            eng.wait_ge(small_in.sem, 16)
            split([wg0[0][:, :], wg0[1][:, :]], col("wg0"))
            split([rw0[0][:, :], rw0[1][:, :]], col("rw0"))
            eng.wait_ge(v_ps.sem, 1)
            eng.wait_ge(c_ps.sem, 1)
            split([wv1[0][:, :], wv1[1][:, :]], two[:, 0, 0:D])
            split([wg1[0][:, D:D + 1], wg1[1][:, D:D + 1]], two[:, 0, D:D + 1])
            step(v.tensor_scalar(score_c[:, :], two[:, 2, 0:1], col("attb"), None, ALU.add))
            v.tensor_tensor(score_c[:, :], two[:, 2, 1:2], score_c[:, :], ALU.add).then_inc(set0_ok.sem, 1)

            def set_up_1():
                v.memset(w3[:, :, :], 0.0)
                v.memset(wg1[0][:, D + 1:D + 2].bitcast(F32), 0.0)
                v.memset(wg1[1][:, D + 1:D + 2].bitcast(F32), 0.0)
                bias_parts(0, "b20", b20[:, :])
                split([wg1[0][:, 0:D], wg1[1][:, 0:D]], col("w1t"))
                split([rw1[0][:, :], rw1[1][:, :]], col("rw1"))
                v.tensor_tensor(mask2[:, :], col("mask"), col("mask"), ALU.mult)
                eng.wait_ge(w0up_in.sem, 16)
                step(v.tensor_copy(w0up[0][:, :], stage_w[:, 0:E0 * H0]))
                v.tensor_tensor(w0up[1][:, :], stage_w[:, 0:E0 * H0], w0up[0][:, :].bitcast(F32), ALU.subtract
                                ).then_inc(set1_ok.sem, 1)

            def set_up_2():
                bias_parts(1, "b21", b21[:, :])
                eng.wait_ge(w1up_in.sem, 16)
                step(v.tensor_copy(w1up[0][:, :], stage_w[:, :]))
                v.tensor_tensor(w1up[1][:, :], stage_w[:, :], w1up[0][:, :].bitcast(F32), ALU.subtract
                                ).then_inc(set2_ok.sem, 1)

            def norm_a(l, g, x):
                for t in range(NT):
                    last = v.bn_stats(st[:, l, t], x[:, t, :])
                last.then_inc(stats[l].sem, 1)
                wait(stats[l], g)
                even, odd = st[:, l, :, 0:3], st[:, l, :, 3:6]
                v.tensor_tensor(mv[:, l, :, 0:2], even[:, :, 1:3], odd[:, :, 1:3], ALU.add)
                v.tensor_tensor(mv[:, l, :, 2], even[:, :, 1], odd[:, :, 1], ALU.subtract
                                ).then_inc(moments[l].sem, 1)
                wait(moments[l], g, 1)
                v.tensor_scalar(mv[:, l, :, 3], mv[:, l, :, 0], 0.5, None, ALU.mult)
                v.scalar_tensor_tensor(mv[:, l, :, 4], mv[:, l, :, 2], 0.25, mv[:, l, :, 2], ALU.mult, ALU.mult)
                v.tensor_scalar(mv[:, l, :, 5], mv[:, l, :, 1], 1.0 / D, LN_EPS, ALU.mult, ALU.add
                                ).then_inc(moments[l].sem, 1)
                wait(moments[l], g, 2)
                v.tensor_tensor(ve[:, l], mv[:, l, :, 4], mv[:, l, :, 5], ALU.add).then_inc(veps[l].sem, 1)

            def norm_b(l, g, x):
                wait(rstd_ok[l], g)
                for t in range(NT):
                    last = v.tensor_scalar(xn[l][:, t, :], x[:, t, :], mv[:, l, t, 3:4], rstd[:, l, t:t + 1],
                                           ALU.subtract, ALU.mult)
                last.then_inc(xn_ok[l].sem, 1)

            def lo(l, g):
                wait(xt_hi[l], g)
                v.tensor_tensor(xt_l[l][:, :], tr[:, :], xt_h[l][:, :].bitcast(F32), ALU.subtract
                                ).then_inc(xt_lo[l].sem, 1)

            def HM(u, f):
                wait(gel_ok, f, u + 1)
                wait(wb_ps, f, u // 2 + 1)
                if u >= 4:
                    wait(dn1_ps, f, u - 3)
                v.tensor_tensor(hm[:, u % 4, :], gel[:, u % 4, :], wb[:, :], ALU.mult).then_inc(hm_ok.sem, 1)

            def unit(n, f):
                kind, u = UNITS[n]
                if kind == "F" and f:
                    if u:
                        HM(u - 1, f)
                    elif not first(f):
                        HM(C1N - 1, before(f))

            def spread(ap, n):
                return ap.unsqueeze(2).to_broadcast([P, NT, n])

            def rows(name, n):
                return col(name).unsqueeze(1).to_broadcast([P, NT, n])

            def result(g):
                wait(yot1_ps, g)
                if not (isinstance(g.pair, int) and number(g) < 2):
                    eng.wait_ge(res_out[g.par].sem, g.pair * 16)
                v.tensor_tensor(res[:, g.par], tr[:, :].rearrange("p (t d) -> p t d", t=NT), x3[:, g.par], ALU.add
                                ).then_inc(res_ok.sem, 1)

            def scores(j, b):
                wait(sgm_ok, b, j + 1)
                v.scalar_tensor_tensor(att[:, j], sgm[:, j], mcur[:, j:j + 1], adj[:, b.par, j], ALU.mult, ALU.mult
                                       ).then_inc(att_ok.sem, 1)

            def attended(b):
                wait(agg1_ps, b)
                v.tensor_tensor(den[:, 0], two[:, :, D], mcur[:, :], ALU.mult).then_inc(den_ok.sem, 1)
                wait(den_ok, b, 1)
                v.tensor_scalar(den[:, 1], den[:, 0], SUM_EPS, None, ALU.add).then_inc(den_ok.sem, 1)
                wait(den_ok, b, 2)
                v.reciprocal(den[:, 2], den[:, 1]).then_inc(den_ok.sem, 1)
                wait(den_ok, b, 3)
                v.tensor_tensor(den[:, 3], den[:, 2], m2cur[:, :], ALU.mult).then_inc(den_ok.sem, 1)
                wait(den_ok, b)
                for t in range(NT):
                    last = v.scalar_tensor_tensor(x3[:, b.par, t], two[:, t, 0:D], den[:, 3, t:t + 1],
                                                  x2[:, b.par, t], ALU.mult, ALU.add)
                last.then_inc(x3_ok.sem, 1)
                wait(x3_ok, b)

            def aggregated(a):
                wait(agg0_ps, a)
                v.tensor_scalar(deg[:, 0], two[:, :, D], SUM_EPS, None, ALU.add).then_inc(deg_ok.sem, 1)
                wait(deg_ok, a, 1)
                v.reciprocal(deg[:, 1], deg[:, 0]).then_inc(deg_ok.sem, 1)
                wait(deg_ok, a)
                for t in range(NT):
                    last = v.scalar_tensor_tensor(usb[:, t], two[:, t, 0:D], deg[:, 1, t:t + 1], zsb[:, t],
                                                  ALU.mult, ALU.add)
                last.then_inc(u_ok.sem, 1)
                wait(u_ok, a)
                v.scalar_tensor_tensor(x1[:, a.par], usb[:, :, :], 0.0, xa[:, a.par], ALU.max, ALU.add
                                       ).then_inc(x1_ok.sem, 1)
                wait(x1_ok, a)

            def best_two(b):
                wait(lg1_ps, b)
                done = [0]

                def step(ins):
                    done[0] += 1
                    ins.then_inc(pick1.sem, 1)
                    wait(pick1, b, done[0])

                step(v.tensor_tensor(lg1[:, :, :], tr[:, 0:NT * E1].rearrange("p (t e) -> p t e", t=NT),
                                     rows("rb1", E1), ALU.add))
                step(v.tensor_reduce(q1[:, 0], lg1[:, :, :], AX_X, ALU.max))
                step(v.tensor_tensor(r1[:, 0], lg1[:, :, :], spread(q1[:, 0], E1), ALU.is_equal))
                step(v.tensor_tensor(r1[:, 1], r1[:, 0], rows("rank1", E1), ALU.mult))
                step(v.tensor_reduce(q1[:, 1], r1[:, 1], AX_X, ALU.max))
                step(v.tensor_tensor(r1[:, 2], r1[:, 1], spread(q1[:, 1], E1), ALU.is_equal))
                step(v.scalar_tensor_tensor(r1[:, 3], r1[:, 2], -OFF, lg1[:, :, :], ALU.mult, ALU.add))
                step(v.tensor_reduce(q1[:, 2], r1[:, 3], AX_X, ALU.max))
                step(v.tensor_tensor(r1[:, 4], r1[:, 3], spread(q1[:, 2], E1), ALU.is_equal))
                step(v.tensor_tensor(r1[:, 5], r1[:, 4], rows("rank1", E1), ALU.mult))
                step(v.tensor_tensor(q1[:, 5], q1[:, 2], q1[:, 0], ALU.subtract))

            def two_weights(b):
                done = [11]

                def step(ins):
                    done[0] += 1
                    ins.then_inc(pick1.sem, 1)
                    wait(pick1, b, done[0])

                step(v.tensor_reduce(q1[:, 3], r1[:, 5], AX_X, ALU.max))
                step(v.tensor_tensor(r1[:, 6], r1[:, 5], spread(q1[:, 3], E1), ALU.is_equal))
                wait(pow1, b)
                step(v.tensor_scalar(q1[:, 7], q1[:, 6], 1.0, None, ALU.add))
                step(v.reciprocal(q1[:, 8], q1[:, 7]))
                step(v.tensor_tensor(r1[:, 7], r1[:, 6], spread(q1[:, 6], E1), ALU.mult))
                step(v.tensor_tensor(r1[:, 8], r1[:, 7], r1[:, 2], ALU.add))
                step(v.tensor_tensor(r1[:, 9], r1[:, 8], spread(q1[:, 8], E1), ALU.mult))
                W = w3[:, :, 0:9 * E1].rearrange("p t (q r e) -> p t q r e", q=3, e=E1)
                step(v.tensor_copy(W[:, :, 0, 0], r1[:, 9]))
                step(v.tensor_tensor(r1[:, 10], r1[:, 9], W[:, :, 0, 0], ALU.subtract))
                v.tensor_copy(W[:, :, 0, 1], r1[:, 10]).then_inc(w3_step.sem, 1)
                wait(w3_step, b, 1)
                v.tensor_tensor(r1[:, 11], r1[:, 10], W[:, :, 0, 1], ALU.subtract).then_inc(w3_step.sem, 1)
                wait(w3_step, b, 2)
                v.tensor_copy(W[:, :, 0, 2], r1[:, 11]).then_inc(w3_step.sem, 1)
                wait(w3_step, b, 3)
                v.tensor_copy(W[:, :, 1], W[:, :, 0])
                step(v.tensor_copy(W[:, :, 2], W[:, :, 0]))

            def best_one(a):
                wait(lg0_ps, a)
                done = [0]

                def step(ins):
                    done[0] += 1
                    ins.then_inc(pick0.sem, 1)
                    wait(pick0, a, done[0])

                step(v.tensor_tensor(lg0[:, :, :], tr[:, 0:NT * E0].rearrange("p (t e) -> p t e", t=NT),
                                      rows("rb0", E0), ALU.add))
                step(v.tensor_reduce(m0[:, 0], lg0[:, :, :], AX_X, ALU.max))
                step(v.tensor_tensor(eq0[:, :, :], lg0[:, :, :], spread(m0[:, 0], E0), ALU.is_equal))
                step(v.tensor_tensor(sc0[:, :, :], eq0[:, :, :], rows("rank0", E0), ALU.mult))
                step(v.tensor_reduce(m0[:, 1], sc0[:, :, :], AX_X, ALU.max))
                S = sel0[:, :, :].rearrange("p t (r e) -> p t r e", e=E0)
                v.tensor_tensor(S[:, :, 0], sc0[:, :, :], spread(m0[:, 1], E0), ALU.is_equal)
                step(v.tensor_tensor(S[:, :, 3], sc0[:, :, :], spread(m0[:, 1], E0), ALU.not_equal))
                v.tensor_copy(S[:, :, 1], S[:, :, 0])
                step(v.tensor_copy(S[:, :, 2], S[:, :, 0]))

            def stage(f, b, k, a, nx):
                unit(0, f)
                if b:
                    lo(2, b)
                if a:
                    lo(0, a)
                unit(2, f)
                if b:
                    wait(h_ps, b)
                    v.tensor_scalar(s2c[:, :], two[:, :, D], score_c[:, 0:1], None, ALU.add).then_inc(s2_ok.sem, 1)
                    v.tensor_tensor(hsb[:, :, 0:D], two[:, :, 0:D], rows("g1row", D), ALU.add
                                    ).then_inc(hsb_ok.sem, 1)
                    v.tensor_copy(mcur[:, :], mask_of(b, col("mask"))).then_inc(mcur_ok.sem, 1)
                    v.tensor_copy(m2cur[:, :], mask_of(b, mask2)).then_inc(mcur_ok.sem, 1)
                unit(4, f)
                if a:
                    wait(y_ps, a)
                    v.tensor_copy(ysb[:, :, 0:D], two[:, :, 0:D])
                    v.tensor_tensor(zsb[:, :, :], two[:, :, D:2 * D], rows("g0row", D), ALU.add
                                    ).then_inc(z_ok.sem, 1)
                if b:
                    wait(mcur_ok, b)
                    eng.wait_ge(adj_in[b.par].sem, (b.pair + 1) * (16 * NT))
                    scores(0, b)
                    scores(1, b)
                unit(6, f)
                if b:
                    scores(2, b)
                    scores(3, b)
                if f and not first(f):
                    result(before(f))
                unit(8, f)
                if b:
                    attended(b)
                    norm_a(3, b, x3[:, b.par])
                unit(10, f)
                if b:
                    norm_b(3, b, x3[:, b.par])
                unit(12, f)
                if a:
                    aggregated(a)
                    norm_a(1, a, x1[:, a.par])
                if b:
                    wait(xt_ps[3], b)
                    v.tensor_scalar(xg[:, :], tr[:, :], col("gamma"), col("beta"), ALU.mult, ALU.add
                                    ).then_inc(xg_ok.sem, 1)
                if a:
                    norm_b(1, a, x1[:, a.par])
                if b:
                    wait(xt_hi[3], b)
                    v.tensor_tensor(xg_l[:, b.par, :], xg[:, :], xg_h[:, b.par, :].bitcast(F32), ALU.subtract
                                    ).then_inc(xt_lo[3].sem, 1)
                unit(14, f)
                if b:
                    best_two(b)
                unit(16, f)
                if a:
                    lo(1, a)
                unit(17, f)
                if b:
                    two_weights(b)
                unit(18, f)
                if a:
                    best_one(a)
                unit(19, f)
                unit(20, f)
                if k:
                    wait(yot0_ps, k)
                    v.tensor_tensor(x2[:, k.par], tr[:, :].rearrange("p (t d) -> p t d", t=NT), x1[:, k.par], ALU.add
                                    ).then_inc(x2_ok.sem, 1)
                    wait(x2_ok, k)
                    norm_a(2, k, x2[:, k.par])
                unit(21, f)
                if nx:
                    eng.wait_ge(x_in[nx.par].sem, (nx.pair + 1) * 16)
                    norm_a(0, nx, xa[:, nx.par])
                if k:
                    norm_b(2, k, x2[:, k.par])
                unit(22, f)
                if nx:
                    norm_b(0, nx, xa[:, nx.par])
                unit(23, f)
                if nx and isinstance(nx.pair, int):
                    if number(nx) == 1:
                        set_up_1()
                    if number(nx) == 2:
                        set_up_2()

            run(stage, eng)
            HM(C1N - 1, graph(G - 1))
            result(graph(G - 1))


def kernel(x, adj, nodemask, L0_gnn_weight, L0_gnn_bias, L0_ffn_router_w, L0_ffn_router_b, L0_ffn_W1, L0_ffn_b1,
           L0_ffn_W2, L0_ffn_b2, L1_gnn_W, L1_gnn_b, L1_gnn_a1, L1_gnn_a2, L1_gnn_att_b, L1_ffn_gamma, L1_ffn_beta,
           L1_ffn_Wr, L1_ffn_br, L1_ffn_W1, L1_ffn_b1, L1_ffn_W2, L1_ffn_b2):
    import concourse.bacc as bacc
    import ml_dtypes
    from concourse.bass_utils import run_bass_kernel_spmd

    f = np.float32

    def row(a):
        return np.broadcast_to(np.asarray(a).reshape(1, -1), (P, np.asarray(a).size))

    def padded(a):
        out = np.zeros((P, a.shape[1]), f)
        out[:a.shape[0]] = a
        return out

    top, bottom = np.split(np.asarray(L0_gnn_weight), 2)
    part = np.zeros((P, 6), f)
    for r in range(3):
        part[r * E0:(r + 1) * E0, r] = 1
        part[r * 3 * E1:(r + 1) * 3 * E1, 3 + r] = 1
    pieces = {
        "wg0": np.concatenate([bottom, top], 1),
        "w1t": np.asarray(L1_gnn_W).T, "w1n": np.asarray(L1_gnn_W),
        "a1a2": np.concatenate([np.repeat(np.asarray(L1_gnn_a1)[:, None], P, 1), np.asarray(L1_gnn_a2)[:, None],
                                np.zeros((P, 1), f)], 1),
        "brep": np.repeat(np.asarray(L1_gnn_b)[:, None], P, 1),
        "rw0": np.asarray(L0_ffn_router_w).T, "rw1": np.asarray(L1_ffn_Wr),
        "b0": np.asarray(L0_ffn_b1).reshape(C0N, P).T, "b1": np.asarray(L1_ffn_b1).reshape(C1N, P).T,
        "gamma": np.asarray(L1_ffn_gamma)[:, None], "beta": np.asarray(L1_ffn_beta)[:, None],
        "attb": row(L1_gnn_att_b),
        "mask": np.asarray(nodemask).reshape(G, NT, P).transpose(2, 0, 1).reshape(P, G * NT),
        "g0row": row(L0_gnn_bias), "g1row": row(L1_gnn_b), "rb0": row(L0_ffn_router_b), "rb1": row(L1_ffn_br),
        "rank0": row(np.arange(E0, 0, -1, dtype=f)), "rank1": row(np.arange(E1, 0, -1, dtype=f)),
        "part": part,
        "b20": padded(np.tile(np.asarray(L0_ffn_b2), (3, 1))),
        "b21": padded(np.tile(np.asarray(L1_ffn_b2), (9, 1))),
        "ident": np.eye(P, dtype=f),
    }
    small = np.ascontiguousarray(np.concatenate([pieces[name] for name, _ in _COLS], 1), f)
    cbf = np.zeros((P, P + (C0N + E1) * P), f)
    cbf[:, :P] = np.eye(P)
    for c in range(C0N):
        for j in range(P):
            cbf[3 * E0 + c * (P // H0) + j // H0, P + c * P + j] = -OFF
    for e in range(E1):
        cbf[[e, E1 + e, 2 * E1 + e], P + (C0N + e) * P:P + (C0N + e + 1) * P] = 1
    arrays = {
        "small": small,
        "cbf": cbf.astype(ml_dtypes.bfloat16),
        "w0up": np.asarray(L0_ffn_W1).transpose(1, 0, 2).reshape(D, E0 * H0),
        "w1up": np.asarray(L1_ffn_W1).transpose(1, 0, 2).reshape(D, E1 * H1),
        "w0dn": np.asarray(L0_ffn_W2).reshape(C0N, P, D).transpose(1, 0, 2),
        "w1dn": np.asarray(L1_ffn_W2).reshape(C1N, P, D).transpose(1, 0, 2),
        "x": np.asarray(x).reshape(G, NT, P, D).transpose(0, 2, 1, 3),
        "adj": np.asarray(adj).transpose(0, 2, 1).reshape(G, NT, P, N).transpose(0, 2, 1, 3),
    }
    arrays = {f"in_{name}": np.ascontiguousarray(a) for name, a in arrays.items()}
    nc = bacc.Bacc("TRN2", target_bir_lowering=False, num_devices=1)
    args = [nc.dram_tensor(name, a.shape, mybir.dt.from_np(a.dtype), kind="ExternalInput").ap()
            for name, a in arrays.items()]
    out = nc.dram_tensor("out", (G, P, NT, D), F32, kind="ExternalOutput").ap()
    build(nc, *args, out)
    r = run_bass_kernel_spmd(nc, [arrays], core_ids=[0])
    return r.results[0]["out"].transpose(0, 2, 1, 3).reshape(G, N, D)
```

```python
from collections import namedtuple
from contextlib import ExitStack

import numpy as np

import concourse.bass as bass
from concourse import mybir

ALU = mybir.AluOpType
ACT = mybir.ActivationFunctionType
F32 = mybir.dt.float32
F32R = mybir.dt.float32r
BF16 = mybir.dt.bfloat16
AX_X = mybir.AxisListType.X

P = 128
G = 16
NT = 4
N = NT * P
D = 128
E0, H0 = 32, 32
E1, H1 = 8, 256
C0N = E0 * H0 // P
C1N = E1 * H1 // P
LN_EPS = 1e-5
SUM_EPS = 1e-8
OFF = 2.0 ** 120
CW = 256
SIGMOIDS = 6
F_LAG = 2
K_LAG = 2
H0BUF = 3
GEL = 4

_COLS = [("wg0", 2 * D), ("w1t", D), ("w1n", D), ("a1a2", D + 2), ("brep", D), ("rw0", E0), ("rw1", E1),
         ("b0", C0N), ("b1", C1N), ("gamma", 1), ("beta", 1), ("attb", 1), ("mask", G * NT),
         ("g0row", D), ("g1row", D), ("rb0", E0), ("rb1", E1), ("rank0", E0), ("rank1", E1),
         ("part", 6), ("b20", D), ("b21", D), ("ident", P)]
COL = {}
_at = 0
for _name, _n in _COLS:
    COL[_name] = (_at, _at + _n)
    _at += _n
SMALL = _at

Graph = namedtuple("Graph", "pair par")


def graph(n):
    return Graph(n // 2, n % 2)


def number(g):
    return g.pair * 2 + g.par


def before(g):
    return Graph(g.pair, 0) if g.par else Graph(g.pair - 1, 1)


class Signal:

    def __init__(self, sem, each=1):
        self.sem, self.each = sem, each

    def after(self, g, k=None):
        k = self.each if k is None else k
        return g.pair * (2 * self.each) + (g.par * self.each + k)


UNITS = [("F", n // 2) if n % 2 == 0 else ("K", n // 2) for n in range(2 * C0N)] + [
    ("F", u) for u in range(C0N, C1N)]


def bank(n, f, k):
    return n % 2 if f and k else UNITS[n][1] % 2


def filling(f):
    return f is None or (isinstance(f.pair, int) and number(f) == 0)


def build(nc, small_d, cbf_d, w0up_d, w1up_d, w0dn_d, w1dn_d, x_d, adj_d, out_d):
    with ExitStack() as ctx:
        def sb(name, shape, dt=F32):
            return ctx.enter_context(nc.sbuf_tensor(name, shape, dt))

        def ps(name, shape, dt=F32):
            return ctx.enter_context(nc.psum_tensor(name, shape, dt))

        def sig(name, each=1):
            return Signal(ctx.enter_context(nc.semaphore(name)), each)

        def sigs(name, n):
            return [sig(f"{name}{i}") for i in range(n)]

        small = sb("small", [P, SMALL])
        cbf = sb("cbf", [P, P + C0N * P], BF16)
        ident_b = cbf[:, 0:P]
        off_w = [cbf[:, P + c * P:P + (c + 1) * P] for c in range(C0N)]

        def col(name, a=None, b=None):
            lo, hi = COL[name]
            return small[:, lo + (a or 0):(hi if b is None else lo + b)]

        stage_w = sb("stage_w", [P, E1 * H1])
        wg0 = [sb(f"wg0_{s}", [P, 2 * D], F32R) for s in "hl"]
        wg1 = [sb(f"wg1_{s}", [P, D + 2], F32R) for s in "hl"]
        wv1 = [sb(f"wv1_{s}", [P, P], F32R) for s in "hl"]
        rw0 = sb("rw0", [P, 2 * E0], F32R)
        w0up = [sb(f"w0up_{s}", [P, E0 * H0], F32R) for s in "hl"]
        w1up = [sb(f"w1up_{s}", [P, E1 * H1], F32R) for s in "hl"]
        w0dn = [sb(f"w0dn_{s}", [P, C0N * D], F32R) for s in "hl"]
        w1dn = sb("w1dn", [P, C1N, D])
        b20 = sb("b20", [P, D], BF16)
        b21 = sb("b21", [P, D], BF16)
        bpart = sb("bpart", [P, 2, 3, D], BF16)
        brest = sb("brest", [P, 2, 2, D])
        bsum = sb("bsum", [P, 2, 2, D])
        half = sb("half", [P, NT])
        warm = sb("warm", [P, 1])
        e_tile = sb("e_tile", [P, NT])
        score_b = sb("score_b", [P, 1])
        score_c = sb("score_c", [P, 1])
        mask2 = sb("mask2", [P, G * NT])
        mcur = sb("mcur", [P, NT])
        m2cur = sb("m2cur", [P, NT])

        xa = sb("xa", [P, 2, NT, D])
        adj0 = sb("adj0", [P, NT, N])
        adj1 = sb("adj1", [P, NT, N])
        x1 = sb("x1", [P, 2, NT, D])
        x2 = sb("x2", [P, 2, NT, D])
        x3 = sb("x3", [P, 2, NT, D])
        res = sb("res", [P, 2, NT, D])
        st = sb("st", [P, 4, NT, 6])
        mv = sb("mv", [P, 4, NT, 6])
        ve = sb("ve", [P, 4, NT])
        rstd = sb("rstd", [P, 4, NT])
        xn = [sb(f"xn{i}", [P, NT, D]) for i in range(3)]
        xn += [xn[1]]
        xt_h = [sb(f"xt_h{i}", [P, 2, N] if i == 1 else [P, 1, N], F32R) for i in range(3)]
        xt_l = [sb(f"xt_l{i}", [P, 2, N] if i == 1 else [P, 1, N], F32R) for i in range(3)]

        def xt(l, g):
            return [x[l][:, g.par if l == 1 else 0, :] for x in (xt_h, xt_l)]

        xg = sb("xg", [P, N])
        xg_h = sb("xg_h", [P, 2, N], F32R)
        xg_l = sb("xg_l", [P, 2, N], F32R)
        ysb = sb("ysb", [P, NT, D + 1])
        zsb = sb("zsb", [P, NT, D])
        usb = sb("usb", [P, NT, D])
        deg = sb("deg", [P, 2, NT])
        lg0_b = sb("lg0_b", [P, NT, E0])
        lg0 = sb("lg0", [P, NT, E0])
        eq0 = sb("eq0", [P, NT, E0])
        sc0 = sb("sc0", [P, NT, E0])
        m0 = sb("m0", [P, 2, NT])
        sel0 = sb("sel0", [P, NT, P], BF16)
        sel0_t = sb("sel0_t", [P, N], BF16)
        h0 = sb("h0", [P, 2, N])
        h0_h = sb("h0_h", [P, H0BUF, N], F32R)
        h0_l = sb("h0_l", [P, H0BUF, N], F32R)
        yo0 = h0[:, 0]
        hsb = sb("hsb", [P, NT, D + 1])
        s2c = sb("s2c", [P, NT])
        sgm = sb("sgm", [P, NT, N])
        att = sgm
        den = sb("den", [P, 4, NT])
        lg1 = sb("lg1", [P, NT, E1])
        r1 = sb("r1", [P, 9, NT, E1])
        q1 = sb("q1", [P, 12, NT])
        wsel = sb("wsel", [P, 2, NT, E1])
        wrest = sb("wrest", [P, 2, NT, E1])
        w3 = sb("w3", [P, NT, P], BF16)
        w3_t = sb("w3_t", [P, N], BF16)
        gel = sb("gel", [P, GEL, N])
        stage_dn = gel[:, 0:2, :].rearrange("p i n -> p (i n)")

        up = [ps(f"up{i}", [P, N]) for i in range(2)]
        y1 = [ps(f"y1_{i}", [P, N]) for i in range(2)]
        two = ps("two", [P, NT, CW])
        tr = ps("tr", [P, N])
        acc0 = ps("acc0", [P, N])
        tr_b = tr[:, 0:N // 2].bitcast(BF16)

        small_in, cbf_in, w0up_in, w1up_in, w0dn_in, w1dn_in = (sig(n) for n in (
            "small_in", "cbf_in", "w0up_in", "w1up_in", "w0dn_in", "w1dn_in"))
        x_in, adj0_in, adj1_in, res_out = (
            sigs("x_in", 2), sig("adj0_in", 16 * NT), sig("adj1_in", 16 * NT), sigs("res_out", 2))
        v_ps, c_ps, set0_ok, set1_ok, set2_ok, set_pool = (
            sig(n) for n in ("v_ps", "c_ps", "set0_ok", "set1_ok", "set2_ok", "set_pool"))
        w0up_hi, w0up_ok, w0dn_hi, w0dn_ok, w1up_hi, w1up_ok = (sig(n) for n in (
            "w0up_hi", "w0up_ok", "w0dn_hi", "w0dn_ok", "w1up_hi", "w1up_ok"))
        stats, veps, rstd_ok, xn_ok, xt_ps = (sigs(n, 4) for n in (
            "stats", "veps", "rstd_ok", "xn_ok", "xt_ps"))
        moments = [sig(f"moments{i}", 2) for i in range(4)]
        xt_hi, xt_lo = sigs("xt_hi", 4), sigs("xt_lo", 4)
        xg_ok = sig("xg_ok")
        y_ps, z_ok = sig("y_ps"), sig("z_ok")
        agg0_ps, deg_ok, u_ok, x1_ok = sig("agg0_ps"), sig("deg_ok", 2), sig("u_ok"), sig("x1_ok")
        lg0_ps, pick0, sel0_ps, sel0_ok = sig("lg0_ps"), sig("pick0", 8), sig("sel0_ps"), sig("sel0_ok")
        up0_ps, h0_ok, h0_lo, dn0_ps, yo0_ok, yot0_ps, x2_ok = (
            sig("up0_ps", C0N), sig("h0_ok", C0N), sig("h0_lo", C0N), sig("dn0_ps", C0N), sig("yo0_ok"),
            sig("yot0_ps"), sig("x2_ok"))
        s1_ps, h_ps, s2_ok, hsb_ok = sig("s1_ps"), sig("h_ps"), sig("s2_ok"), sig("hsb_ok")
        sgm_ok, att_ok, agg1_ps, den_ok, x3_ok = (
            sig("sgm_ok", NT), sig("att_ok", NT), sig("agg1_ps"), sig("den_ok", 4), sig("x3_ok"))
        lg1_ps, pick1, pow1 = sig("lg1_ps"), sig("pick1", 18), sig("pow1")
        up1_ps, gel_ok, dn1_ps, res_ok = (
            sig("up1_ps", C1N), sig("gel_ok", C1N), sig("dn1_ps", C1N), sig("res_ok", E1 + 1))
        w3_step, w3_ps, w3_ok, bias1_ps = sig("w3_step", 5), sig("w3_ps"), sig("w3_ok"), sig("bias1_ps")
        set_step, mcur_ok = sig("set_step"), sig("mcur_ok", 2)
        SET_POOL = 4

        block = ctx.enter_context(nc.Block())

        def run(stage, eng):
            def at(f):
                stage(*[graph(n) if 0 <= n < G else None for n in range(f, f + 5)])

            for f in range(-4, 3):
                at(f)
            with eng.Fori(1, 1 + (G - 8) // 2) as i:
                stage(Graph(i, 1), Graph(i + 1, 0), Graph(i + 1, 1), Graph(i + 2, 0), Graph(i + 2, 1))
                stage(Graph(i + 1, 0), Graph(i + 1, 1), Graph(i + 2, 0), Graph(i + 2, 1), Graph(i + 3, 0))
            for f in range(G - 5, G):
                at(f)

        @block.sync
        def _(eng):
            def wait(s, g, k=None):
                eng.wait_ge(s.sem, s.after(g, k))

            def load_x(g):
                eng.dma_start(xa[:, g.par], x_d[bass.ds(number(g), 1)].rearrange("g p t d -> p (g t) d")
                              ).then_inc(x_in[g.par].sem, 16)

            def load_adj(buf, g, j, done):
                eng.dma_start(buf[:, j], adj_d[bass.ds(number(g), 1), :, j].rearrange("g p n -> p (g n)")
                              ).then_inc(done.sem, 16)

            def store(g):
                wait(res_ok, g)
                eng.dma_start(out_d[bass.ds(number(g), 1)].rearrange("g p t d -> p (g t) d"), res[:, g.par]
                              ).then_inc(res_out[g.par].sem, 16)

            load_x(graph(0))
            eng.dma_start(small[:, :], small_d).then_inc(small_in.sem, 16)
            for j in range(NT):
                load_adj(adj0, graph(0), j, adj0_in)
            load_x(graph(1))
            eng.dma_start(cbf[:, :], cbf_d).then_inc(cbf_in.sem, 16)
            eng.dma_start(stage_w[:, 0:E0 * H0], w0up_d).then_inc(w0up_in.sem, 16)
            eng.dma_start(stage_dn, w0dn_d).then_inc(w0dn_in.sem, 16)
            eng.wait_ge(w0up_ok.sem, 1)
            eng.dma_start(stage_w[:, :], w1up_d).then_inc(w1up_in.sem, 16)
            eng.dma_start(w1dn[:, :, :], w1dn_d).then_inc(w1dn_in.sem, 16)

            def stage(f, b, k, a, nx):
                if f and not (isinstance(f.pair, int) and number(f) == 0):
                    store(before(f))
                if k:
                    for j in range(NT):
                        if b:
                            wait(att_ok, b, j + 1)
                        load_adj(adj1, k, j, adj1_in)
                if a and nx:
                    wait(agg0_ps, a)
                    for j in range(NT):
                        load_adj(adj0, nx, j, adj0_in)
                if a and number_after(a, 2) is not None:
                    wait(x1_ok, a)
                    load_x(number_after(a, 2))

            def number_after(g, n):
                if isinstance(g.pair, int) and number(g) + n >= G:
                    return None
                return Graph(g.pair + n // 2, g.par)

            run(stage, eng)
            store(graph(G - 1))
            for par in range(2):
                eng.wait_ge(res_out[par].sem, 16 * (G // 2))

        @block.gpsimd
        def _(eng):
            def wait(s, g, k=None):
                eng.wait_ge(s.sem, s.after(g, k))

            def first(g):
                return isinstance(g.pair, int) and number(g) == 0

            eng.memset(half[:, :], -0.5).then_inc(set_pool.sem, 1)
            eng.memset(e_tile[:, :], float(np.e)).then_inc(set_pool.sem, 1)
            eng.memset(ysb[:, :, D:D + 1], 1.0).then_inc(set_pool.sem, 1)
            eng.memset(hsb[:, :, D:D + 1], 1.0).then_inc(set_pool.sem, 1)
            eng.wait_ge(set_pool.sem, SET_POOL)

            def inv_std(l, g):
                wait(veps[l], g)
                eng.tensor_tensor(rstd[:, l], ve[:, l], half[:, :], ALU.pow).then_inc(rstd_ok[l].sem, 1)

            def hidden0(k, *chunks):
                for u in chunks:
                    if k:
                        wait(h0_ok, k, u + 1)
                        if u >= H0BUF:
                            wait(dn0_ps, k, u - H0BUF + 1)
                        elif not first(k):
                            wait(dn0_ps, before(k))
                        eng.tensor_tensor(h0_l[:, u % H0BUF, :], h0[:, u % 2, :], h0_h[:, u % H0BUF, :].bitcast(F32),
                                          ALU.subtract).then_inc(h0_lo.sem, 1)

            def stage(f, b, k, a, nx):
                hidden0(k, 0, 1)
                if b and first(b):
                    eng.wait_ge(w1up_hi.sem, 1)
                    eng.tensor_tensor(w1up[1][:, :], stage_w[:, :], w1up[0][:, :].bitcast(F32), ALU.subtract
                                      ).then_inc(w1up_ok.sem, 1)
                hidden0(k, 2)
                if nx:
                    inv_std(0, nx)
                if a and first(a):
                    eng.wait_ge(w0up_hi.sem, 1)
                    eng.tensor_tensor(w0up[1][:, :], stage_w[:, 0:E0 * H0], w0up[0][:, :].bitcast(F32), ALU.subtract
                                      ).then_inc(w0up_ok.sem, 1)
                hidden0(k, 3)
                if a:
                    inv_std(1, a)
                if a and first(a):
                    eng.wait_ge(w0dn_hi.sem, 1)
                    eng.tensor_tensor(w0dn[1][:, :], stage_dn, w0dn[0][:, :].bitcast(F32), ALU.subtract
                                      ).then_inc(w0dn_ok.sem, 1)
                hidden0(k, 4, 5)
                if b:
                    inv_std(3, b)
                hidden0(k, 6, 7)
                if b:
                    wait(pick1, b, 11)
                    eng.tensor_tensor(q1[:, 6], e_tile[:, :], q1[:, 5], ALU.pow).then_inc(pow1.sem, 1)
                if k:
                    inv_std(2, k)

            run(stage, eng)

        @block.tensor
        def _(eng):
            mm = nc.tensor.matmul

            def wait(s, g, k=None):
                eng.wait_ge(s.sem, s.after(g, k))

            def three(out, lhs, rhs, start, stop):
                mm(out, lhs[0], rhs[0], start=start, stop=False)
                mm(out, lhs[0], rhs[1], start=False, stop=False)
                return mm(out, lhs[1], rhs[0], start=False, stop=stop)

            eng.wait_ge(small_in.sem, 16)
            mm(y1[0][:, 0:D + 2], col("w1n"), col("a1a2"), start=True, stop=True).then_inc(v_ps.sem, 1)
            mm(y1[1][:, 0:2], col("brep"), col("a1a2", D - 1, D + 1), start=True, stop=True).then_inc(c_ps.sem, 1)
            eng.wait_ge(set_pool.sem, SET_POOL)

            def first(g):
                return isinstance(g.pair, int) and number(g) == 0

            def turn(l, g, t_free):
                wait(xn_ok[l], g)
                for what in t_free:
                    wait(*what)
                for t in range(NT):
                    last = nc.tensor.transpose(tr[:, t * P:(t + 1) * P], xn[l][:, t, :], col("ident"))
                last.then_inc(xt_ps[l].sem, 1)

            def project0(g, two_free):
                wait(xt_hi[0], g)
                wait(xt_lo[0], g)
                for s, h in two_free:
                    wait(s, h)
                for t in range(NT):
                    x = [h[:, t * P:(t + 1) * P] for h in xt(0, g)]
                    last = three(two[:, t, 0:2 * D], x, [wg0[0][:, :], wg0[1][:, :]], True, True)
                last.then_inc(y_ps.sem, 1)

            def gather(g, weights, values, done):
                for t in range(NT):
                    for k in range(NT):
                        last = mm(two[:, t, 0:D + 1], weights[:, k, t * P:(t + 1) * P], values[:, k, :],
                                  start=(k == 0), stop=(k == NT - 1))
                last.then_inc(done.sem, 1)

            def route0(a):
                for t in range(NT):
                    at = t * 2 * E0
                    x = [h[:, t * P:(t + 1) * P] for h in xt(1, a)]
                    mm(tr[:, at:at + 2 * E0], x[0], rw0[:, :], start=True, stop=False)
                    last = mm(tr[:, at:at + E0], x[1], rw0[:, 0:E0], start=False, stop=True)
                last.then_inc(lg0_ps.sem, 1)

            def route1(b):
                for t in range(NT):
                    last = mm(tr[:, t * E1:(t + 1) * E1], xg[:, t * P:(t + 1) * P], col("rw1"), start=True, stop=True)
                last.then_inc(lg1_ps.sem, 1)

            def turn_b(src, done):
                for t in range(NT):
                    last = nc.tensor.transpose(tr_b[:, t * P:(t + 1) * P], src[:, t, :], ident_b)
                last.then_inc(done.sem, 1)

            def up_free(n, f, k):
                kind, u = UNITS[n]
                if f is None:
                    if u >= 2:
                        wait(h0_ok, k, u - 1)
                elif k is None:
                    if u >= 2:
                        wait(gel_ok, f, u - 1)
                    elif not first(f):
                        wait(gel_ok, before(f), C1N - 1 + u)
                elif n < 2:
                    if not first(f):
                        wait(gel_ok, before(f), C1N + n - 1)
                elif UNITS[n - 2][0] == "F":
                    wait(gel_ok, f, UNITS[n - 2][1] + 1)
                else:
                    wait(h0_ok, k, UNITS[n - 2][1] + 1)

            def back(g, src, done):
                for t in range(NT):
                    last = nc.tensor.transpose(tr[:, t * P:(t + 1) * P], src[:, t * P:(t + 1) * P], col("ident"))
                last.then_inc(done.sem, 1)

            def k_down(c, k):
                if c == 0:
                    if not first(k):
                        wait(yo0_ok, before(k))
                    mm(acc0[:, :], b20[:, :], sel0_t[:, :], start=True, stop=False)
                    if first(k):
                        eng.wait_ge(w0dn_ok.sem, 1)
                wait(h0_ok, k, c + 1)
                wait(h0_lo, k, c + 1)
                w = [w0dn[0][:, c * D:(c + 1) * D], w0dn[1][:, c * D:(c + 1) * D]]
                three(acc0[:, :], w, [h0_h[:, c % H0BUF, :], h0_l[:, c % H0BUF, :]], False, c == C0N - 1
                      ).then_inc(dn0_ps.sem, 1)

            def f_down(u, f):
                e = u // 2
                if u % 2 == 0:
                    if e >= 2:
                        wait(res_ok, f, e - 1 if e == 2 else e)
                    elif not first(f):
                        wait(res_ok, before(f), E1 + e)
                wait(gel_ok, f, u + 1)
                for t in range(NT):
                    last = mm(y1[e % 2][:, t * P:(t + 1) * P], gel[:, u % GEL, t * P:(t + 1) * P], w1dn[:, u, :],
                              start=(u % 2 == 0 and t == 0), stop=(u % 2 == 1 and t == NT - 1))
                last.then_inc(dn1_ps.sem, 1)

            def unit(n, f, k):
                kind, u = UNITS[n]
                if kind == "K":
                    if k:
                        up_free(n, f, k)
                        w = [w0up[0][:, u * P:(u + 1) * P], w0up[1][:, u * P:(u + 1) * P]]
                        three(up[bank(n, f, k)][:, :], w, xt(1, k), True, False)
                        if u == 0:
                            wait(sel0_ok, k)
                        mm(up[bank(n, f, k)][:, :], off_w[u], sel0_t[:, :], start=False, stop=True
                           ).then_inc(up0_ps.sem, 1)
                        if u >= K_LAG and n != SIGMOIDS + 1:
                            k_down(u - K_LAG, k)
                    return
                prev = before(f) if f and not first(f) else None

                def down():
                    if u < F_LAG:
                        if prev:
                            f_down(C1N - F_LAG + u, prev)
                    elif f:
                        f_down(u - F_LAG, f)

                early = n == SIGMOIDS
                if early:
                    down()
                    if k:
                        k_down(UNITS[n + 1][1] - K_LAG, k)
                if f:
                    if u == 0:
                        wait(xt_hi[3], f)
                        wait(xt_lo[3], f)
                    up_free(n, f, k)
                    w = [w1up[0][:, u * P:(u + 1) * P], w1up[1][:, u * P:(u + 1) * P]]
                    three(up[bank(n, f, k)][:, :], w, [xg_h[:, f.par, :], xg_l[:, f.par, :]], True, True
                          ).then_inc(up1_ps.sem, 1)
                if not early:
                    down()

            def stage(f, b, k, a, nx):
                if a and first(a):
                    eng.wait_ge(set0_ok.sem, 1)
                if k and first(k):
                    eng.wait_ge(set1_ok.sem, 1)
                    eng.wait_ge(w0up_ok.sem, 1)
                if f and first(f):
                    eng.wait_ge(set2_ok.sem, 1)
                    eng.wait_ge(w1up_ok.sem, 1)
                    eng.wait_ge(w1dn_in.sem, 16)
                late = filling(f) and b
                if late:
                    for n in range(4):
                        unit(n, f, k)
                if b:
                    turn(2, b, [(x2_ok, b)])
                if not late:
                    unit(0, f, k)
                if a:
                    turn(0, a, [(xt_lo[2], b)] if b else [(sel0_ok, k)] if k else [])
                if not late:
                    unit(1, f, k)
                    unit(2, f, k)
                if b:
                    wait(xt_hi[2], b)
                    wait(xt_lo[2], b)
                    if a:
                        wait(xt_lo[0], a)
                    three(tr[:, :], [wv1[0][:, :], wv1[1][:, :]], xt(2, b), True, True
                          ).then_inc(s1_ps.sem, 1)
                    for t in range(NT):
                        x = [h[:, t * P:(t + 1) * P] for h in xt(2, b)]
                        last = three(two[:, t, 0:D + 2], x, [wg1[0][:, :], wg1[1][:, :]], True, True)
                    last.then_inc(h_ps.sem, 1)
                if not late:
                    unit(3, f, k)
                unit(4, f, k)
                if a:
                    project0(a, [(hsb_ok, b), (s2_ok, b)] if b else [])
                unit(5, f, k)
                if a:
                    wait(z_ok, a)
                    wait(adj0_in, a)
                    gather(a, adj0, ysb, agg0_ps)
                unit(6, f, k)
                if f:
                    if b:
                        wait(sgm_ok, b)
                    wait(w3_step, f)
                    turn_b(w3, w3_ps)
                unit(7, f, k)
                unit(8, f, k)
                if f:
                    wait(w3_ok, f)
                    for t in range(NT):
                        last = mm(tr[:, t * P:(t + 1) * P], w3_t[:, t * P:(t + 1) * P], b21[:, :],
                                  start=True, stop=True)
                    last.then_inc(bias1_ps.sem, 1)
                if b:
                    if a:
                        wait(u_ok, a)
                    wait(att_ok, b)
                    gather(b, att, hsb, agg1_ps)
                unit(9, f, k)
                unit(10, f, k)
                second = k and not b
                if second:
                    for n in range(11, 14):
                        unit(n, f, k)
                s1_read = [(res_ok, f, 2)] if f else [(sgm_ok, b)] if b else []
                if a:
                    turn(1, a, s1_read)
                if second:
                    for n in range(14, 16):
                        unit(n, f, k)
                else:
                    unit(11, f, k)
                    unit(12, f, k)
                if a:
                    wait(xt_hi[1], a)
                    wait(xt_lo[1], a)
                    if first(a):
                        eng.wait_ge(set1_ok.sem, 1)
                    route0(a)
                if not second:
                    unit(13, f, k)
                    unit(14, f, k)
                if b:
                    turn(3, b, [(pick0, a, 2)] if a else s1_read)
                if not second:
                    unit(15, f, k)
                unit(16, f, k)
                if b:
                    wait(xg_ok, b)
                    route1(b)
                if k:
                    k_down(C0N - 2, k)
                unit(17, f, k)
                if k:
                    k_down(C0N - 1, k)
                if a:
                    wait(pick0, a)
                    if b:
                        wait(pick1, b, 1)
                    if first(a):
                        eng.wait_ge(cbf_in.sem, 16)
                    turn_b(sel0, sel0_ps)
                unit(18, f, k)
                if k:
                    wait(yo0_ok, k)
                    if a:
                        wait(sel0_ok, a)
                    elif b:
                        wait(pick1, b, 1)
                    back(k, yo0, yot0_ps)
                for n in range(19, 24):
                    unit(n, f, k)

            run(stage, eng)
            for u in range(C1N - F_LAG, C1N):
                f_down(u, graph(G - 1))

        @block.scalar
        def _(eng):
            act = nc.scalar.activation

            def wait(s, g, k=None):
                eng.wait_ge(s.sem, s.after(g, k))

            eng.wait_ge(small_in.sem, 16)
            act(warm[:, :], col("attb"), ACT.Gelu)

            def first(g):
                return isinstance(g.pair, int) and number(g) == 0

            def hi(l, g):
                wait(xt_ps[l], g)
                act(xt(l, g)[0], tr[:, :], ACT.Copy).then_inc(xt_hi[l].sem, 1)

            def unit(n, f, k):
                kind, u = UNITS[n]
                if kind == "K":
                    if k:
                        wait(up0_ps, k, u + 1)
                        if u >= 2:
                            wait(h0_lo, k, u - 1)
                        elif not first(k):
                            wait(yot0_ps, before(k))
                        act(h0[:, u % 2, :], up[bank(n, f, k)][:, :], ACT.Relu, bias=col("b0", u, u + 1))
                        if u >= H0BUF:
                            wait(dn0_ps, k, u - H0BUF + 1)
                        act(h0_h[:, u % H0BUF, :], up[bank(n, f, k)][:, :], ACT.Relu, bias=col("b0", u, u + 1)
                            ).then_inc(h0_ok.sem, 1)
                elif f:
                    wait(up1_ps, f, u + 1)
                    if u >= GEL:
                        wait(dn1_ps, f, u - GEL + 1)
                    elif not first(f):
                        wait(dn1_ps, before(f), C1N + u - GEL + 1)
                    act(gel[:, u % GEL, :], up[bank(n, f, k)][:, :], ACT.Gelu, bias=col("b1", u, u + 1)
                        ).then_inc(gel_ok.sem, 1)

            def stage(f, b, k, a, nx):
                late = filling(f) and b
                if late:
                    for n in range(4):
                        unit(n, f, k)
                if b:
                    hi(2, b)
                if not late:
                    unit(0, f, k)
                if a:
                    hi(0, a)
                if a and first(a):
                    eng.wait_ge(w0up_in.sem, 16)
                    act(w0up[0][:, :], stage_w[:, 0:E0 * H0], ACT.Copy).then_inc(w0up_hi.sem, 1)
                    eng.wait_ge(w0dn_in.sem, 16)
                    act(w0dn[0][:, :], stage_dn, ACT.Copy).then_inc(w0dn_hi.sem, 1)
                if not late:
                    for n in range(1, 4):
                        unit(n, f, k)
                if b:
                    wait(s2_ok, b)
                    wait(s1_ps, b)
                    if not first(b):
                        wait(agg1_ps, before(b))
                    for j in range(NT):
                        act(sgm[:, j, :], tr[:, :], ACT.Sigmoid, bias=s2c[:, j:j + 1]).then_inc(sgm_ok.sem, 1)
                for n in range(4, 11):
                    unit(n, f, k)
                    if n == 5 and k and first(k):
                        eng.wait_ge(w1up_in.sem, 16)
                        act(w1up[0][:, :], stage_w[:, :], ACT.Copy).then_inc(w1up_hi.sem, 1)
                    if n == 6 and f:
                        wait(w3_ps, f)
                        act(w3_t[:, :], tr_b, ACT.Copy).then_inc(w3_ok.sem, 1)
                cut = 14 if k and not b else 11
                for n in range(11, cut):
                    unit(n, f, k)
                if a:
                    hi(1, a)
                for n in range(cut, 16):
                    unit(n, f, k)
                if b:
                    wait(xg_ok, b)
                    act(xg_h[:, b.par, :], xg[:, :], ACT.Copy).then_inc(xt_hi[3].sem, 1)
                unit(16, f, k)
                unit(17, f, k)
                if k:
                    wait(dn0_ps, k)
                    act(yo0, acc0[:, :], ACT.Relu).then_inc(yo0_ok.sem, 1)
                if a:
                    wait(sel0_ps, a)
                    act(sel0_t[:, :], tr_b, ACT.Copy).then_inc(sel0_ok.sem, 1)
                for n in range(18, 24):
                    unit(n, f, k)

            run(stage, eng)

        @block.vector
        def _(eng):
            v = nc.vector

            def wait(s, g, k=None):
                eng.wait_ge(s.sem, s.after(g, k))

            def first(g):
                return isinstance(g.pair, int) and number(g) == 0

            step_n = [0]

            def step(ins):
                step_n[0] += 1
                ins.then_inc(set_step.sem, 1)
                eng.wait_ge(set_step.sem, step_n[0])

            def split(pair, src):
                step(v.tensor_copy(pair[0], src))
                step(v.tensor_tensor(pair[1], src, pair[0].bitcast(F32), ALU.subtract))

            def bias_parts(n, name, out, done):
                def rows_of(r):
                    return col("part", 3 * n + r, 3 * n + r + 1)

                step(v.tensor_copy(bpart[:, n, 0], col(name)))
                step(v.tensor_tensor(brest[:, n, 0], col(name), bpart[:, n, 0], ALU.subtract))
                step(v.tensor_copy(bpart[:, n, 1], brest[:, n, 0]))
                step(v.tensor_tensor(brest[:, n, 1], brest[:, n, 0], bpart[:, n, 1], ALU.subtract))
                step(v.tensor_copy(bpart[:, n, 2], brest[:, n, 1]))
                step(v.tensor_scalar(bsum[:, n, 0], bpart[:, n, 0], rows_of(0), None, ALU.mult))
                step(v.scalar_tensor_tensor(bsum[:, n, 1], bpart[:, n, 1], rows_of(1), bsum[:, n, 0],
                                            ALU.mult, ALU.add))
                v.scalar_tensor_tensor(out, bpart[:, n, 2], rows_of(2), bsum[:, n, 1], ALU.mult, ALU.add
                                       ).then_inc(done.sem, 1)

            def mask_of(g, m):
                return m[:, bass.ds(number(g) * NT, NT)]

            def set_up_0():
                eng.wait_ge(small_in.sem, 16)
                step(v.tensor_copy(wg0[0][:, :], col("wg0")))
                v.tensor_tensor(wg0[1][:, :], col("wg0"), wg0[0][:, :].bitcast(F32), ALU.subtract
                                ).then_inc(set0_ok.sem, 1)

            def set_up_1():
                split([rw0[:, 0:E0], rw0[:, E0:2 * E0]], col("rw0"))
                v.memset(w3[:, :, :], 0.0)
                v.memset(wg1[0][:, D + 1:D + 2].bitcast(F32), 0.0)
                v.memset(wg1[1][:, D + 1:D + 2].bitcast(F32), 0.0)
                split([wg1[0][:, 0:D], wg1[1][:, 0:D]], col("w1t"))
                eng.wait_ge(v_ps.sem, 1)
                split([wv1[0][:, :], wv1[1][:, :]], y1[0][:, 0:D])
                split([wg1[0][:, D:D + 1], wg1[1][:, D:D + 1]], y1[0][:, D:D + 1])
                eng.wait_ge(c_ps.sem, 1)
                step(v.tensor_scalar(score_b[:, :], y1[1][:, 0:1], col("attb"), None, ALU.add))
                v.tensor_tensor(score_c[:, :], y1[1][:, 1:2], score_b[:, :], ALU.add)
                v.tensor_tensor(mask2[:, :], col("mask"), col("mask"), ALU.mult)

            def set_up_b20():
                bias_parts(0, "b20", b20[:, :], set1_ok)

            def set_up_2():
                bias_parts(1, "b21", b21[:, :], set2_ok)

            def norm_a(l, g, x):
                for t in range(NT):
                    last = v.bn_stats(st[:, l, t], x[:, t, :])
                last.then_inc(stats[l].sem, 1)
                wait(stats[l], g)
                even, odd = st[:, l, :, 0:3], st[:, l, :, 3:6]
                v.tensor_tensor(mv[:, l, :, 0:2], even[:, :, 1:3], odd[:, :, 1:3], ALU.add)
                v.tensor_tensor(mv[:, l, :, 2], even[:, :, 1], odd[:, :, 1], ALU.subtract
                                ).then_inc(moments[l].sem, 1)
                wait(moments[l], g, 1)
                v.tensor_scalar(mv[:, l, :, 3], mv[:, l, :, 0], 0.5, None, ALU.mult)
                v.scalar_tensor_tensor(mv[:, l, :, 4], mv[:, l, :, 2], 0.25, mv[:, l, :, 2], ALU.mult, ALU.mult)
                v.tensor_scalar(mv[:, l, :, 5], mv[:, l, :, 1], 1.0 / D, LN_EPS, ALU.mult, ALU.add
                                ).then_inc(moments[l].sem, 1)
                wait(moments[l], g, 2)
                v.tensor_tensor(ve[:, l], mv[:, l, :, 4], mv[:, l, :, 5], ALU.add).then_inc(veps[l].sem, 1)

            def norm_b(l, g, x):
                wait(rstd_ok[l], g)
                for t in range(NT):
                    last = v.tensor_scalar(xn[l][:, t, :], x[:, t, :], mv[:, l, t, 3:4], rstd[:, l, t:t + 1],
                                           ALU.subtract, ALU.mult)
                last.then_inc(xn_ok[l].sem, 1)

            def lo(l, g):
                wait(xt_hi[l], g)
                high, low = xt(l, g)
                v.tensor_tensor(low, tr[:, :], high.bitcast(F32), ALU.subtract
                                ).then_inc(xt_lo[l].sem, 1)

            def weighted(e, f):
                wait(dn1_ps, f, 2 * e + 2)
                if e:
                    wait(res_ok, f, e + 1)
                elif not (isinstance(f.pair, int) and number(f) < 2):
                    eng.wait_ge(res_out[f.par].sem, f.pair * 16)
                for t in range(NT):
                    last = v.scalar_tensor_tensor(
                        res[:, f.par, t], y1[e % 2][:, t * P:(t + 1) * P], wsel[:, f.par, t, e:e + 1],
                        (res if e else x3)[:, f.par, t], ALU.mult, ALU.add)
                last.then_inc(res_ok.sem, 1)

            def bias1(f):
                wait(bias1_ps, f)
                wait(res_ok, f, 1)
                v.tensor_tensor(res[:, f.par], tr[:, :].rearrange("p (t d) -> p t d", t=NT), res[:, f.par], ALU.add
                                ).then_inc(res_ok.sem, 1)

            def sum_up(n, f):
                kind, u = UNITS[n]
                e = (u - F_LAG - 2) // 2
                if kind == "F" and f and (u - F_LAG) % 2 == 0:
                    if e >= 0:
                        weighted(e, f)
                    elif not first(f):
                        weighted(E1 + e, before(f))

            def spread(ap, n):
                return ap.unsqueeze(2).to_broadcast([P, NT, n])

            def rows(name, n):
                return col(name).unsqueeze(1).to_broadcast([P, NT, n])

            def scores(j, b):
                wait(sgm_ok, b, j + 1)
                v.scalar_tensor_tensor(att[:, j], sgm[:, j], mcur[:, j:j + 1], adj1[:, j], ALU.mult, ALU.mult
                                       ).then_inc(att_ok.sem, 1)

            def attended(b):
                wait(agg1_ps, b)
                v.tensor_tensor(den[:, 0], two[:, :, D], mcur[:, :], ALU.mult).then_inc(den_ok.sem, 1)
                wait(den_ok, b, 1)
                v.tensor_scalar(den[:, 1], den[:, 0], SUM_EPS, None, ALU.add).then_inc(den_ok.sem, 1)
                wait(den_ok, b, 2)
                v.reciprocal(den[:, 2], den[:, 1]).then_inc(den_ok.sem, 1)
                wait(den_ok, b, 3)
                v.tensor_tensor(den[:, 3], den[:, 2], m2cur[:, :], ALU.mult).then_inc(den_ok.sem, 1)
                wait(den_ok, b)
                for t in range(NT):
                    last = v.scalar_tensor_tensor(x3[:, b.par, t], two[:, t, 0:D], den[:, 3, t:t + 1],
                                                  x2[:, b.par, t], ALU.mult, ALU.add)
                last.then_inc(x3_ok.sem, 1)
                wait(x3_ok, b)

            def aggregated(a):
                wait(agg0_ps, a)
                v.tensor_scalar(deg[:, 0], two[:, :, D], SUM_EPS, None, ALU.add).then_inc(deg_ok.sem, 1)
                wait(deg_ok, a, 1)
                v.reciprocal(deg[:, 1], deg[:, 0]).then_inc(deg_ok.sem, 1)
                wait(deg_ok, a)
                for t in range(NT):
                    last = v.scalar_tensor_tensor(usb[:, t], two[:, t, 0:D], deg[:, 1, t:t + 1], zsb[:, t],
                                                  ALU.mult, ALU.add)
                last.then_inc(u_ok.sem, 1)
                wait(u_ok, a)
                v.scalar_tensor_tensor(x1[:, a.par], usb[:, :, :], 0.0, xa[:, a.par], ALU.max, ALU.add
                                       ).then_inc(x1_ok.sem, 1)
                wait(x1_ok, a)

            def logits1(b):
                wait(lg1_ps, b)
                v.tensor_tensor(lg1[:, :, :], tr[:, 0:NT * E1].rearrange("p (t e) -> p t e", t=NT),
                                rows("rb1", E1), ALU.add).then_inc(pick1.sem, 1)

            def best_two(b):
                done = [1]

                def step(ins):
                    done[0] += 1
                    ins.then_inc(pick1.sem, 1)
                    wait(pick1, b, done[0])

                wait(pick1, b, 1)
                step(v.tensor_reduce(q1[:, 0], lg1[:, :, :], AX_X, ALU.max))
                step(v.tensor_tensor(r1[:, 0], lg1[:, :, :], spread(q1[:, 0], E1), ALU.is_equal))
                step(v.tensor_tensor(r1[:, 1], r1[:, 0], rows("rank1", E1), ALU.mult))
                step(v.tensor_reduce(q1[:, 1], r1[:, 1], AX_X, ALU.max))
                step(v.tensor_tensor(r1[:, 2], r1[:, 1], spread(q1[:, 1], E1), ALU.is_equal))
                step(v.scalar_tensor_tensor(r1[:, 3], r1[:, 2], -OFF, lg1[:, :, :], ALU.mult, ALU.add))
                step(v.tensor_reduce(q1[:, 2], r1[:, 3], AX_X, ALU.max))
                step(v.tensor_tensor(r1[:, 4], r1[:, 3], spread(q1[:, 2], E1), ALU.is_equal))
                step(v.tensor_tensor(r1[:, 5], r1[:, 4], rows("rank1", E1), ALU.mult))
                step(v.tensor_tensor(q1[:, 5], q1[:, 2], q1[:, 0], ALU.subtract))

            def two_weights(f):
                done = [11]

                def step(ins):
                    done[0] += 1
                    ins.then_inc(pick1.sem, 1)
                    wait(pick1, f, done[0])

                step(v.tensor_reduce(q1[:, 3], r1[:, 5], AX_X, ALU.max))
                step(v.tensor_tensor(r1[:, 6], r1[:, 5], spread(q1[:, 3], E1), ALU.is_equal))
                wait(pow1, f)
                step(v.tensor_scalar(q1[:, 7], q1[:, 6], 1.0, None, ALU.add))
                step(v.reciprocal(q1[:, 8], q1[:, 7]))
                step(v.tensor_tensor(r1[:, 7], r1[:, 6], spread(q1[:, 6], E1), ALU.mult))
                step(v.tensor_tensor(r1[:, 8], r1[:, 7], r1[:, 2], ALU.add))
                step(v.tensor_tensor(wsel[:, f.par], r1[:, 8], spread(q1[:, 8], E1), ALU.mult))

            def weight_parts(f):
                done = [0]

                def step(ins):
                    done[0] += 1
                    ins.then_inc(w3_step.sem, 1)
                    if done[0] < 5:
                        wait(w3_step, f, done[0])

                W = w3[:, :, 0:9 * E1].rearrange("p t (q r e) -> p t q r e", q=3, e=E1)
                v.tensor_copy(W[:, :, 0, 0], wsel[:, f.par])
                v.tensor_copy(W[:, :, 1, 0], wsel[:, f.par])
                step(v.tensor_copy(W[:, :, 2, 0], wsel[:, f.par]))
                step(v.tensor_tensor(wrest[:, 0], wsel[:, f.par], W[:, :, 0, 0], ALU.subtract))
                v.tensor_copy(W[:, :, 0, 1], wrest[:, 0])
                v.tensor_copy(W[:, :, 1, 1], wrest[:, 0])
                step(v.tensor_copy(W[:, :, 2, 1], wrest[:, 0]))
                step(v.tensor_tensor(wrest[:, 1], wrest[:, 0], W[:, :, 0, 1], ALU.subtract))
                v.tensor_copy(W[:, :, 0, 2], wrest[:, 1])
                v.tensor_copy(W[:, :, 1, 2], wrest[:, 1])
                step(v.tensor_copy(W[:, :, 2, 2], wrest[:, 1]))

            def best_one(a):
                wait(lg0_ps, a)
                done = [0]

                def step(ins):
                    done[0] += 1
                    ins.then_inc(pick0.sem, 1)
                    wait(pick0, a, done[0])

                halves = tr[:, 0:NT * 2 * E0].rearrange("p (t i e) -> p t i e", t=NT, i=2)
                step(v.tensor_tensor(lg0_b[:, :, :], halves[:, :, 0], rows("rb0", E0), ALU.add))
                step(v.tensor_tensor(lg0[:, :, :], halves[:, :, 1], lg0_b[:, :, :], ALU.add))
                step(v.tensor_reduce(m0[:, 0], lg0[:, :, :], AX_X, ALU.max))
                step(v.tensor_tensor(eq0[:, :, :], lg0[:, :, :], spread(m0[:, 0], E0), ALU.is_equal))
                step(v.tensor_tensor(sc0[:, :, :], eq0[:, :, :], rows("rank0", E0), ALU.mult))
                step(v.tensor_reduce(m0[:, 1], sc0[:, :, :], AX_X, ALU.max))
                S = sel0[:, :, :].rearrange("p t (r e) -> p t r e", e=E0)
                v.tensor_tensor(S[:, :, 0], sc0[:, :, :], spread(m0[:, 1], E0), ALU.is_equal)
                step(v.tensor_tensor(S[:, :, 3], sc0[:, :, :], spread(m0[:, 1], E0), ALU.not_equal))
                v.tensor_copy(S[:, :, 1], S[:, :, 0])
                step(v.tensor_copy(S[:, :, 2], S[:, :, 0]))

            def stage(f, b, k, a, nx):
                if b:
                    lo(2, b)
                sum_up(0, f)
                if a:
                    lo(0, a)
                if a and first(a):
                    set_up_1()
                if k and first(k):
                    set_up_2()
                if b:
                    v.tensor_copy(mcur[:, :], mask_of(b, col("mask"))).then_inc(mcur_ok.sem, 1)
                    v.tensor_copy(m2cur[:, :], mask_of(b, mask2)).then_inc(mcur_ok.sem, 1)
                    wait(h_ps, b)
                    v.tensor_scalar(s2c[:, :], two[:, :, D], score_c[:, 0:1], None, ALU.add).then_inc(s2_ok.sem, 1)
                    v.tensor_tensor(hsb[:, :, 0:D], two[:, :, 0:D], rows("g1row", D), ALU.add
                                    ).then_inc(hsb_ok.sem, 1)
                if f:
                    two_weights(f)
                    weight_parts(f)
                if a:
                    wait(y_ps, a)
                    v.tensor_copy(ysb[:, :, 0:D], two[:, :, 0:D])
                    v.tensor_tensor(zsb[:, :, :], two[:, :, D:2 * D], rows("g0row", D), ALU.add
                                    ).then_inc(z_ok.sem, 1)
                sum_up(4, f)
                if b:
                    wait(mcur_ok, b)
                    wait(adj1_in, b)
                    for j in range(NT):
                        scores(j, b)
                if a and first(a):
                    set_up_b20()
                if nx:
                    eng.wait_ge(x_in[nx.par].sem, (nx.pair + 1) * 16)
                    norm_a(0, nx, xa[:, nx.par])
                    if first(nx):
                        set_up_0()
                        norm_b(0, nx, xa[:, nx.par])
                if a:
                    aggregated(a)
                    norm_a(1, a, x1[:, a.par])
                sum_up(8, f)
                if nx and not first(nx):
                    norm_b(0, nx, xa[:, nx.par])
                if a:
                    norm_b(1, a, x1[:, a.par])
                if f:
                    bias1(f)
                if b:
                    attended(b)
                    norm_a(3, b, x3[:, b.par])
                sum_up(12, f)
                if a:
                    lo(1, a)
                if b:
                    norm_b(3, b, x3[:, b.par])
                if a:
                    best_one(a)
                if b:
                    wait(xt_ps[3], b)
                    v.tensor_scalar(xg[:, :], tr[:, :], col("gamma"), col("beta"), ALU.mult, ALU.add
                                    ).then_inc(xg_ok.sem, 1)
                sum_up(16, f)
                if b:
                    wait(xt_hi[3], b)
                    v.tensor_tensor(xg_l[:, b.par, :], xg[:, :], xg_h[:, b.par, :].bitcast(F32), ALU.subtract
                                    ).then_inc(xt_lo[3].sem, 1)
                if b:
                    logits1(b)
                    best_two(b)
                sum_up(18, f)
                if k:
                    wait(yot0_ps, k)
                    v.tensor_tensor(x2[:, k.par], tr[:, :].rearrange("p (t d) -> p t d", t=NT), x1[:, k.par], ALU.add
                                    ).then_inc(x2_ok.sem, 1)
                    wait(x2_ok, k)
                    norm_a(2, k, x2[:, k.par])
                sum_up(20, f)
                sum_up(22, f)
                if k:
                    norm_b(2, k, x2[:, k.par])

            run(stage, eng)
            for e in range(E1 - F_LAG // 2 - 1, E1):
                weighted(e, graph(G - 1))


def kernel(x, adj, nodemask, L0_gnn_weight, L0_gnn_bias, L0_ffn_router_w, L0_ffn_router_b, L0_ffn_W1, L0_ffn_b1,
           L0_ffn_W2, L0_ffn_b2, L1_gnn_W, L1_gnn_b, L1_gnn_a1, L1_gnn_a2, L1_gnn_att_b, L1_ffn_gamma, L1_ffn_beta,
           L1_ffn_Wr, L1_ffn_br, L1_ffn_W1, L1_ffn_b1, L1_ffn_W2, L1_ffn_b2):
    import concourse.bacc as bacc
    import ml_dtypes
    from concourse.bass_utils import run_bass_kernel_spmd

    f = np.float32

    def row(a):
        return np.broadcast_to(np.asarray(a).reshape(1, -1), (P, np.asarray(a).size))

    def padded(a):
        out = np.zeros((P, a.shape[1]), f)
        out[:a.shape[0]] = a
        return out

    top, bottom = np.split(np.asarray(L0_gnn_weight), 2)
    part = np.zeros((P, 6), f)
    for r in range(3):
        part[r * E0:(r + 1) * E0, r] = 1
        part[r * 3 * E1:(r + 1) * 3 * E1, 3 + r] = 1
    pieces = {
        "wg0": np.concatenate([bottom, top], 1),
        "w1t": np.asarray(L1_gnn_W).T, "w1n": np.asarray(L1_gnn_W),
        "a1a2": np.concatenate([np.repeat(np.asarray(L1_gnn_a1)[:, None], P, 1), np.asarray(L1_gnn_a2)[:, None],
                                np.zeros((P, 1), f)], 1),
        "brep": np.repeat(np.asarray(L1_gnn_b)[:, None], P, 1),
        "rw0": np.asarray(L0_ffn_router_w).T, "rw1": np.asarray(L1_ffn_Wr),
        "b0": np.asarray(L0_ffn_b1).reshape(C0N, P).T, "b1": np.asarray(L1_ffn_b1).reshape(C1N, P).T,
        "gamma": np.asarray(L1_ffn_gamma)[:, None], "beta": np.asarray(L1_ffn_beta)[:, None],
        "attb": row(L1_gnn_att_b),
        "mask": np.asarray(nodemask).reshape(G, NT, P).transpose(2, 0, 1).reshape(P, G * NT),
        "g0row": row(L0_gnn_bias), "g1row": row(L1_gnn_b), "rb0": row(L0_ffn_router_b), "rb1": row(L1_ffn_br),
        "rank0": row(np.arange(E0, 0, -1, dtype=f)), "rank1": row(np.arange(E1, 0, -1, dtype=f)),
        "part": part,
        "b20": padded(np.tile(np.asarray(L0_ffn_b2), (3, 1))),
        "b21": padded(np.tile(np.asarray(L1_ffn_b2), (9, 1))),
        "ident": np.eye(P, dtype=f),
    }
    small = np.ascontiguousarray(np.concatenate([pieces[name] for name, _ in _COLS], 1), f)
    cbf = np.zeros((P, P + C0N * P), f)
    cbf[:, :P] = np.eye(P)
    for c in range(C0N):
        for j in range(P):
            cbf[3 * E0 + c * (P // H0) + j // H0, P + c * P + j] = -OFF
    arrays = {
        "small": small,
        "cbf": cbf.astype(ml_dtypes.bfloat16),
        "w0up": np.asarray(L0_ffn_W1).transpose(1, 0, 2).reshape(D, E0 * H0),
        "w1up": np.asarray(L1_ffn_W1).transpose(1, 0, 2).reshape(D, E1 * H1),
        "w0dn": np.asarray(L0_ffn_W2).reshape(C0N, P, D).transpose(1, 0, 2).reshape(P, C0N * D),
        "w1dn": np.asarray(L1_ffn_W2).reshape(C1N, P, D).transpose(1, 0, 2),
        "x": np.asarray(x).reshape(G, NT, P, D).transpose(0, 2, 1, 3),
        "adj": np.asarray(adj).transpose(0, 2, 1).reshape(G, NT, P, N).transpose(0, 2, 1, 3),
    }
    arrays = {f"in_{name}": np.ascontiguousarray(a) for name, a in arrays.items()}
    nc = bacc.Bacc("TRN2", target_bir_lowering=False, num_devices=1)
    args = [nc.dram_tensor(name, a.shape, mybir.dt.from_np(a.dtype), kind="ExternalInput").ap()
            for name, a in arrays.items()]
    out = nc.dram_tensor("out", (G, P, NT, D), F32, kind="ExternalOutput").ap()
    build(nc, *args, out)
    r = run_bass_kernel_spmd(nc, [arrays], core_ids=[0])
    return r.results[0]["out"].transpose(0, 2, 1, 3).reshape(G, N, D)
```
